# Optimizing a Trainium2 kernel written in Bass

```python
import numpy as np
import jax
import jax.numpy as jnp

def _softmax(x, axis=-1):
    return jax.nn.softmax(x, axis=axis)

def _gelu(x):
    return jax.nn.gelu(x, approximate=True)

def _silu(x):
    return jax.nn.silu(x)

def _sigmoid(x):
    return jax.nn.sigmoid(x)

def _layernorm(x, axis=-1, eps=1e-05):
    m = jnp.mean(x, axis=axis, keepdims=True)
    v = jnp.var(x, axis=axis, keepdims=True)
    return (x - m) / jnp.sqrt(v + eps)

def _scatter_add(tgt, idx, src, axis=0):
    return tgt.at[idx].add(src)

def _segment_sum(src, seg, n):
    return jax.ops.segment_sum(src, seg, n)
kernel_name = 'mk_lm_tower_d1_tok_ids256_r4_b7be50'

def setup_inputs(seed: int=0):
    np.random.seed(seed)
    _w = jnp.asarray

    def _rec_inputs():
        import jax
        import jax.numpy as jnp
        _rk = jax.random.key(seed)
        x = jax.random.randint(jax.random.fold_in(_rk, 1), (2, 2048), 0, 127998, jnp.int32)
        return x
    x = _rec_inputs()

    def _L0_tok_setup():
        import jax, jax.numpy as jnp
        import numpy as np
        VOCAB = 32000
        HIDDEN = 512
        BATCH, SEQ = (4, 1024)
        key = jax.random.key(seed)
        k_ids, k_tab = jax.random.split(key)
        input_ids = jax.random.randint(k_ids, (BATCH, SEQ), 0, VOCAB, dtype=jnp.int32)
        ple_table = jax.random.normal(k_tab, (VOCAB, HIDDEN), dtype=jnp.float32)
        return {'input_ids': input_ids, 'ple_table': ple_table, 'layer_idx': 3, 'ple_dim': 64}
    _L0_tok_all = _L0_tok_setup()
    _L0_tok_in = {k: v for k, v in _L0_tok_all.items() if k in ('ple_table',)}
    del _L0_tok_all

    def _L0_attn_setup():
        import jax, jax.numpy as jnp
        import numpy as np
        from functools import partial
        B, L, DM = (4, 1024, 64)
        DH = DM * 2
        N = 16
        K = 4
        R = DH // 16
        EPS = 1e-05

        def silu(x):
            return x * jax.nn.sigmoid(x)

        def layernorm(x, g, b):
            m = jnp.mean(x, -1, keepdims=True)
            v = jnp.var(x, -1, keepdims=True)
            return (x - m) * jax.lax.rsqrt(v + EPS) * g + b

        def dwconv_causal(x, w, b):
            xt = jnp.transpose(x, (0, 2, 1))
            y = jax.lax.conv_general_dilated(xt, w[:, None, :], window_strides=(1,), padding=[(w.shape[1] - 1, 0)], dimension_numbers=('NCH', 'OIH', 'NCH'), feature_group_count=xt.shape[1])
            return jnp.transpose(y, (0, 2, 1)) + b

        def selective_scan(u, dt, Bm, Cm, A, Dp):

            def step(h, inp):
                u_t, dt_t, B_t, C_t = inp
                dA = jnp.exp(dt_t[..., None] * A)
                h = h * dA + (dt_t * u_t)[..., None] * B_t[:, None, :]
                y = jnp.einsum('bdn,bn->bd', h, C_t)
                return (h, y)
            h0 = jnp.zeros((u.shape[0], u.shape[2], A.shape[1]), u.dtype)
            xs = (jnp.swapaxes(u, 0, 1), jnp.swapaxes(dt, 0, 1), jnp.swapaxes(Bm, 0, 1), jnp.swapaxes(Cm, 0, 1))
            _, ys = jax.lax.scan(step, h0, xs)
            return jnp.swapaxes(ys, 0, 1) + u * Dp

        def mamba(u, in_w, conv_w, conv_b, xproj_w, dt_w, dt_b, A_log, Dp, out_w):
            xz = u @ in_w.T
            x, z = jnp.split(xz, 2, axis=-1)
            x = silu(dwconv_causal(x, conv_w, conv_b))
            x_dbl = x @ xproj_w.T
            dt = jax.nn.softplus(x_dbl[..., :R] @ dt_w.T + dt_b)
            Bm = x_dbl[..., R:R + N]
            Cm = x_dbl[..., R + N:]
            A = -jnp.exp(A_log)
            y = selective_scan(x, dt, Bm, Cm, A, Dp)
            return y * silu(z) @ out_w.T
        key = jax.random.key(seed)
        ks = iter(jax.random.split(key, 32))
        rn = lambda *s: jax.random.normal(next(ks), s, jnp.float32) * 0.02
        d = {'x': jax.random.normal(next(ks), (B, L, DM), jnp.float32)}
        d['ln_g'] = jnp.ones((DM,), jnp.float32)
        d['ln_b'] = jnp.zeros((DM,), jnp.float32)
        d['in_w'] = rn(2 * DH, DM)
        d['conv_w'] = rn(DH, K)
        d['conv_b'] = jnp.zeros((DH,), jnp.float32)
        d['out_w'] = rn(DM, 2 * DH)
        A_log0 = jnp.log(jnp.tile(jnp.arange(1, N + 1, dtype=jnp.float32), (DH, 1)))
        for p in ('f', 'b'):
            d[p + '_in_w'] = rn(2 * DH, DH)
            d[p + '_conv_w'] = rn(DH, K)
            d[p + '_conv_b'] = jnp.zeros((DH,), jnp.float32)
            d[p + '_xproj_w'] = rn(R + 2 * N, DH)
            d[p + '_dt_w'] = rn(DH, R)
            d[p + '_dt_b'] = rn(DH)
            d[p + '_Alog'] = A_log0
            d[p + '_D'] = jnp.ones((DH,), jnp.float32)
            d[p + '_out_w'] = rn(DH, DH)
        return d
    _L0_attn_all = _L0_attn_setup()
    _L0_attn_in = {k: v for k, v in _L0_attn_all.items() if k in ('ln_g', 'ln_b', 'in_w', 'conv_w', 'conv_b', 'out_w', 'f_in_w', 'f_conv_w', 'f_conv_b', 'f_xproj_w', 'f_dt_w', 'f_dt_b', 'f_Alog', 'f_D', 'f_out_w', 'b_in_w', 'b_conv_w', 'b_conv_b', 'b_xproj_w', 'b_dt_w', 'b_dt_b', 'b_Alog', 'b_D', 'b_out_w')}
    del _L0_attn_all

    def _L0_ffn_setup():
        import jax, jax.numpy as jnp
        import numpy as np
        B, K, D = (128, 16, 64)
        E = 32
        H = int(D * 0.25)
        key = jax.random.key(seed)
        ks = jax.random.split(key, 7)
        d_rs = D ** (-0.5)
        h_rs = H ** (-0.5)
        x = jax.random.normal(ks[0], (B, K, D), dtype=jnp.float32)
        router_w = jax.random.uniform(ks[1], (E, D), jnp.float32, -d_rs, d_rs)
        router_b = jax.random.uniform(ks[2], (E,), jnp.float32, -d_rs, d_rs)
        W1 = jax.random.uniform(ks[3], (E, D, H), jnp.float32, -h_rs, h_rs)
        b1 = jax.random.uniform(ks[4], (E, H), jnp.float32, -h_rs, h_rs)
        W2 = jax.random.uniform(ks[5], (E, H, D), jnp.float32, -d_rs, d_rs)
        b2 = jax.random.uniform(ks[6], (E, D), jnp.float32, -d_rs, d_rs)
        return {'x': x, 'router_w': router_w, 'router_b': router_b, 'W1': W1, 'b1': b1, 'W2': W2, 'b2': b2}
    _L0_ffn_all = _L0_ffn_setup()
    _L0_ffn_in = {k: v for k, v in _L0_ffn_all.items() if k in ('router_w', 'router_b', 'W1', 'b1', 'W2', 'b2')}
    del _L0_ffn_all
    return {'x': x, 'L0_tok_ple_table': _L0_tok_in['ple_table'], 'L0_attn_ln_g': _L0_attn_in['ln_g'], 'L0_attn_ln_b': _L0_attn_in['ln_b'], 'L0_attn_in_w': _L0_attn_in['in_w'], 'L0_attn_conv_w': _L0_attn_in['conv_w'], 'L0_attn_conv_b': _L0_attn_in['conv_b'], 'L0_attn_out_w': _L0_attn_in['out_w'], 'L0_attn_f_in_w': _L0_attn_in['f_in_w'], 'L0_attn_f_conv_w': _L0_attn_in['f_conv_w'], 'L0_attn_f_conv_b': _L0_attn_in['f_conv_b'], 'L0_attn_f_xproj_w': _L0_attn_in['f_xproj_w'], 'L0_attn_f_dt_w': _L0_attn_in['f_dt_w'], 'L0_attn_f_dt_b': _L0_attn_in['f_dt_b'], 'L0_attn_f_Alog': _L0_attn_in['f_Alog'], 'L0_attn_f_D': _L0_attn_in['f_D'], 'L0_attn_f_out_w': _L0_attn_in['f_out_w'], 'L0_attn_b_in_w': _L0_attn_in['b_in_w'], 'L0_attn_b_conv_w': _L0_attn_in['b_conv_w'], 'L0_attn_b_conv_b': _L0_attn_in['b_conv_b'], 'L0_attn_b_xproj_w': _L0_attn_in['b_xproj_w'], 'L0_attn_b_dt_w': _L0_attn_in['b_dt_w'], 'L0_attn_b_dt_b': _L0_attn_in['b_dt_b'], 'L0_attn_b_Alog': _L0_attn_in['b_Alog'], 'L0_attn_b_D': _L0_attn_in['b_D'], 'L0_attn_b_out_w': _L0_attn_in['b_out_w'], 'L0_ffn_router_w': _L0_ffn_in['router_w'], 'L0_ffn_router_b': _L0_ffn_in['router_b'], 'L0_ffn_W1': _L0_ffn_in['W1'], 'L0_ffn_b1': _L0_ffn_in['b1'], 'L0_ffn_W2': _L0_ffn_in['W2'], 'L0_ffn_b2': _L0_ffn_in['b2']}

def reference(x, L0_tok_ple_table, L0_attn_ln_g, L0_attn_ln_b, L0_attn_in_w, L0_attn_conv_w, L0_attn_conv_b, L0_attn_out_w, L0_attn_f_in_w, L0_attn_f_conv_w, L0_attn_f_conv_b, L0_attn_f_xproj_w, L0_attn_f_dt_w, L0_attn_f_dt_b, L0_attn_f_Alog, L0_attn_f_D, L0_attn_f_out_w, L0_attn_b_in_w, L0_attn_b_conv_w, L0_attn_b_conv_b, L0_attn_b_xproj_w, L0_attn_b_dt_w, L0_attn_b_dt_b, L0_attn_b_Alog, L0_attn_b_D, L0_attn_b_out_w, L0_ffn_router_w, L0_ffn_router_b, L0_ffn_W1, L0_ffn_b1, L0_ffn_W2, L0_ffn_b2):
    import jax
    import jax.numpy as jnp

    def _L0_tok_ref(input_ids, ple_table, layer_idx, ple_dim):
        import jax, jax.numpy as jnp
        import numpy as np
        VOCAB = 32000
        HIDDEN = 512
        BATCH, SEQ = (4, 1024)
        start = layer_idx * ple_dim
        layer_slice = jax.lax.dynamic_slice_in_dim(ple_table, start, ple_dim, axis=1)
        return layer_slice[input_ids].astype(jnp.float32)

    def _L0_attn_ref(x, ln_g, ln_b, in_w, conv_w, conv_b, out_w, f_in_w, f_conv_w, f_conv_b, f_xproj_w, f_dt_w, f_dt_b, f_Alog, f_D, f_out_w, b_in_w, b_conv_w, b_conv_b, b_xproj_w, b_dt_w, b_dt_b, b_Alog, b_D, b_out_w):
        import jax, jax.numpy as jnp
        import numpy as np
        from functools import partial
        B, L, DM = (4, 1024, 64)
        DH = DM * 2
        N = 16
        K = 4
        R = DH // 16
        EPS = 1e-05

        def silu(x):
            return x * jax.nn.sigmoid(x)

        def layernorm(x, g, b):
            m = jnp.mean(x, -1, keepdims=True)
            v = jnp.var(x, -1, keepdims=True)
            return (x - m) * jax.lax.rsqrt(v + EPS) * g + b

        def dwconv_causal(x, w, b):
            xt = jnp.transpose(x, (0, 2, 1))
            y = jax.lax.conv_general_dilated(xt, w[:, None, :], window_strides=(1,), padding=[(w.shape[1] - 1, 0)], dimension_numbers=('NCH', 'OIH', 'NCH'), feature_group_count=xt.shape[1])
            return jnp.transpose(y, (0, 2, 1)) + b

        def selective_scan(u, dt, Bm, Cm, A, Dp):

            def step(h, inp):
                u_t, dt_t, B_t, C_t = inp
                dA = jnp.exp(dt_t[..., None] * A)
                h = h * dA + (dt_t * u_t)[..., None] * B_t[:, None, :]
                y = jnp.einsum('bdn,bn->bd', h, C_t)
                return (h, y)
            h0 = jnp.zeros((u.shape[0], u.shape[2], A.shape[1]), u.dtype)
            xs = (jnp.swapaxes(u, 0, 1), jnp.swapaxes(dt, 0, 1), jnp.swapaxes(Bm, 0, 1), jnp.swapaxes(Cm, 0, 1))
            _, ys = jax.lax.scan(step, h0, xs)
            return jnp.swapaxes(ys, 0, 1) + u * Dp

        def mamba(u, in_w, conv_w, conv_b, xproj_w, dt_w, dt_b, A_log, Dp, out_w):
            xz = u @ in_w.T
            x, z = jnp.split(xz, 2, axis=-1)
            x = silu(dwconv_causal(x, conv_w, conv_b))
            x_dbl = x @ xproj_w.T
            dt = jax.nn.softplus(x_dbl[..., :R] @ dt_w.T + dt_b)
            Bm = x_dbl[..., R:R + N]
            Cm = x_dbl[..., R + N:]
            A = -jnp.exp(A_log)
            y = selective_scan(x, dt, Bm, Cm, A, Dp)
            return y * silu(z) @ out_w.T
        residual = x
        h = layernorm(x, ln_g, ln_b)
        proj = h @ in_w.T
        conv_input, gate = jnp.split(proj, 2, axis=-1)
        act = silu(dwconv_causal(conv_input, conv_w, conv_b))
        fwd = mamba(act, f_in_w, f_conv_w, f_conv_b, f_xproj_w, f_dt_w, f_dt_b, f_Alog, f_D, f_out_w)
        rev = jnp.flip(act, axis=1)
        bwd = jnp.flip(mamba(rev, b_in_w, b_conv_w, b_conv_b, b_xproj_w, b_dt_w, b_dt_b, b_Alog, b_D, b_out_w), axis=1)
        mamba_out = jnp.concatenate([fwd, bwd], axis=-1)
        gated = mamba_out * silu(jnp.concatenate([gate, gate], axis=-1))
        return gated @ out_w.T + residual

    def _L0_ffn_ref(x, router_w, router_b, W1, b1, W2, b2):
        import jax, jax.numpy as jnp
        import numpy as np
        B, K, D = (128, 16, 64)
        E = 32
        H = int(D * 0.25)
        xf = x.reshape(-1, D)
        logits = xf @ router_w.T + router_b
        idx = jnp.argmax(logits, axis=-1)
        w1t = jnp.take(W1, idx, axis=0)
        h = jnp.einsum('nd,ndh->nh', xf, w1t) + jnp.take(b1, idx, axis=0)
        h = jax.nn.relu(h)
        w2t = jnp.take(W2, idx, axis=0)
        out = jnp.einsum('nh,nhd->nd', h, w2t) + jnp.take(b2, idx, axis=0)
        out = jax.nn.relu(out)
        return out.reshape(x.shape)
    h = _L0_tok_ref(x, L0_tok_ple_table, 3, 64)
    h = h + _L0_attn_ref(_layernorm(h, axis=-1), L0_attn_ln_g, L0_attn_ln_b, L0_attn_in_w, L0_attn_conv_w, L0_attn_conv_b, L0_attn_out_w, L0_attn_f_in_w, L0_attn_f_conv_w, L0_attn_f_conv_b, L0_attn_f_xproj_w, L0_attn_f_dt_w, L0_attn_f_dt_b, L0_attn_f_Alog, L0_attn_f_D, L0_attn_f_out_w, L0_attn_b_in_w, L0_attn_b_conv_w, L0_attn_b_conv_b, L0_attn_b_xproj_w, L0_attn_b_dt_w, L0_attn_b_dt_b, L0_attn_b_Alog, L0_attn_b_D, L0_attn_b_out_w)
    h = h + _L0_ffn_ref(_layernorm(h, axis=-1), L0_ffn_router_w, L0_ffn_router_b, L0_ffn_W1, L0_ffn_b1, L0_ffn_W2, L0_ffn_b2)
    return h

_drawn_inputs = setup_inputs


def setup_inputs(seed=0):
    import zlib

    import numpy as np

    out = dict(_drawn_inputs(seed))
    spreads = {'L0_attn_ln_g': (1.0, 0.6),
     'L0_attn_ln_b': (0.0, 0.8),
     'L0_attn_conv_b': (0.0, 0.8),
     'L0_attn_f_conv_b': (0.0, 0.8),
     'L0_attn_f_D': (1.0, 0.6),
     'L0_attn_b_conv_b': (0.0, 0.8),
     'L0_attn_b_D': (1.0, 0.6)}
    factors = {'L0_attn_in_w': 8.0,
     'L0_attn_conv_w': 8.0,
     'L0_attn_out_w': 8.0,
     'L0_attn_f_in_w': 8.0,
     'L0_attn_f_conv_w': 8.0,
     'L0_attn_f_xproj_w': 8.0,
     'L0_attn_f_Alog': 8.0,
     'L0_attn_f_out_w': 8.0,
     'L0_attn_b_in_w': 8.0,
     'L0_attn_b_conv_w': 8.0,
     'L0_attn_b_xproj_w': 8.0,
     'L0_attn_b_Alog': 8.0,
     'L0_attn_b_out_w': 8.0,
     'L0_ffn_b1': 44.64,
     'L0_attn_f_dt_w': 7.55,
     'L0_attn_f_dt_b': 8.0,
     'L0_attn_b_dt_w': 3.067,
     'L0_attn_b_dt_b': 6.783,
     'L0_ffn_router_w': 6.034,
     'L0_ffn_router_b': 8.0,
     'L0_ffn_W1': 6.837,
     'L0_ffn_W2': 6.08,
     'L0_ffn_b2': 22.903}
    for name, (base, spread) in spreads.items():
        noise = np.random.default_rng([zlib.crc32(name.encode()), seed]).standard_normal(out[name].shape)
        drawn = base * np.exp(spread * noise) if base else spread * noise
        out[name] = jnp.asarray(drawn.astype(out[name].dtype))
    for name, factor in factors.items():
        out[name] = (out[name] * factor).astype(out[name].dtype)
    return out
```

```python
from contextlib import ExitStack

import numpy as np

import concourse.bass as bass
from concourse import mybir
from concourse.alu_op_type import AluOpType as ALU

ACT = mybir.ActivationFunctionType
F32 = mybir.dt.float32
BF16 = mybir.dt.bfloat16
I32 = mybir.dt.int32
AX = mybir.AxisListType.X

P = 128
T = 512
NQ = 4
NR = 4
BIG = float(2.0 ** 120)
EPS = 1e-5
REV = slice(None, None, -1)


class Chain:

    def __init__(self, eng, sem):
        self.eng, self.sem, self.base, self.k = eng, sem, 0, 0

    def mark(self, ins):
        ins.then_inc(self.sem, 1)
        self.k += 1

    def wait(self):
        self.eng.wait_ge(self.sem, self.base + self.k)

    def step(self, ins):
        self.mark(ins)
        self.wait()

    def loop(self, start, end, body):
        base, k0 = self.base, self.k
        per = self._per(body)
        with self.eng.Fori(start, end) as i:
            self.base, self.k = base + k0 + (i - start) * per, 0
            body(i)
            assert self.k == per
        self.base, self.k = base, k0 + (end - start) * per

    def _per(self, body):
        return body.marks


def marks(n):
    def put(body):
        body.marks = n
        return body
    return put


def build(nc, ins, out):
    x, table = ins["x"], ins["L0_tok_ple_table"]
    B, L = x.shape
    V, HID = table.shape
    DM = ins["L0_attn_ln_g"].shape[0]
    DH = ins["L0_attn_conv_w"].shape[0]
    NS = ins["L0_attn_f_Alog"].shape[1]
    R = ins["L0_attn_f_dt_w"].shape[1]
    E, _, H = ins["L0_ffn_W1"].shape
    SLICE = 3
    NTOK = B * L
    TILES = NTOK // P
    TB = TILES // B
    TC = T // P
    NCH = NTOK // T
    CB = L // T
    NBLK = E * H // P
    UNITS = 2 * NCH
    DIRS = ("f", "b")
    assert DH == P and NQ * 32 == DH and NR * 4 == NS and 2 * DM == P

    with ExitStack() as ctx:
        def sb(name, shape, dt=F32):
            return ctx.enter_context(nc.sbuf_tensor(name, shape, dt))

        sems = {}

        def sem(name):
            if name not in sems:
                sems[name] = ctx.enter_context(nc.semaphore(name))
            return sems[name]

        ps = ctx.enter_context(nc.psum_tensor("ps", [P, 8, T], F32))
        bc_dram = nc.dram_tensor("bc_dram", (2, 2 * NS, NTOK), F32, kind="Internal").ap()

        ident = sb("ident", [P, P])
        spread = sb("spread", [P, NQ, P])
        fold = sb("fold", [P, 32])
        wT = sb("wT", [P, 16, P])
        gate_wT = sb("gate_wT", [DM, P])
        router_wT = sb("router_wT", [DM + 1, E])
        dt_wT = sb("dt_wT", [R, 2, P])
        dtproj = sb("dtproj", [P, 2, P])
        skip = sb("skip", [P, 2, P])
        negA = sb("negA", [P, 2, NQ, NR])
        dt_b = sb("dt_b", [P, 2])
        conv_b = sb("conv_b", [P, 3])
        ln_g = sb("ln_g", [P, 1])
        ln_b = sb("ln_b", [P, 1])
        eps = sb("eps", [P, 1])
        w1 = sb("w1", [DM, E, H])
        b1 = sb("b1", [P, NBLK])
        w2 = sb("w2", [P, NBLK, DM])
        b2 = sb("b2", [E, DM])
        pick = sb("pick", [E + 1, NBLK, P], BF16)
        rank = sb("rank", [P, E])
        carry = sb("carry", [P, 2, NQ, NR])
        lns = sb("lns", [P, 8, TB])
        x0 = sb("x0", [P, TILES, DM])
        u = sb("u", [P, TILES, DM])
        gate = sb("gate", [P, NTOK])
        xs = sb("xs", [P, 2, NTOK])
        z = sb("z", [P, 2, NTOK])
        arena = sb("arena", [P, 89 * 256])

        def carve(at, *shape, rows=P, dt=F32):
            n = int(np.prod(shape))
            v = arena[0:rows, at:at + n]
            if len(shape) > 1:
                names = "abcd"[:len(shape)]
                v = v.rearrange(f"p ({' '.join(names)}) -> p {' '.join(names)}",
                                **{k: s for k, s in zip(names, shape)})
            return v, at + n

        PADW = L + 6
        uT, a = carve(0, B, PADW)
        act, a = carve(a, B, PADW)
        u2d, a = carve(a, TB, 2, DM)
        xc, a = carve(a, TB, DM)
        sq, a = carve(a, TB, DM)
        bc_sb, a = carve(a, 2, T, rows=2 * NS)
        REP_AT = 57 * 256
        assert a <= REP_AT
        in_w, a = carve(REP_AT, 2, DM)
        conv_w, a = carve(a, 3, 4)
        dir_w, a = carve(a, 2, 2, P)
        taps, a = carve(a, 2, 2, DM)
        dir_taps, a = carve(a, 2, 4, P)
        xbc, a = carve(a, 2, P, rows=2 * NS)
        xdt, a = carve(a, 2, P, rows=R)
        dt_w, a = carve(a, 2, R)
        dskip, a = carve(a, 2)
        dir_ow, a = carve(a, 2, P)
        out_w, a = carve(a, 4 * DM, rows=DM)
        router_w, a = carve(a, DM, rows=E)
        alog, a = carve(a, 2, NQ, NS)
        pickf, a = carve(a, NBLK, P, rows=E + 1)
        idx_f, a = carve(a, P, rows=TILES)
        idx_g, a = carve(a, P, rows=TILES)
        assert a <= 89 * 256
        ids = sb("ids", [TILES, P], I32)
        idx = sb("idx", [P, TILES], I32)
        ranki = sb("ranki", [P, E], I32)
        act_r, a = carve(REP_AT, B, PADW)
        assert a <= 89 * 256
        rep, a = carve(REP_AT, 2, 2, NR, T)
        assert a <= 89 * 256
        v_, a = carve(0, T)
        e_, a = carve(a, T)
        w_, a = carve(a, T)
        l_, a = carve(a, T)
        dt, a = carve(a, 2, T)
        du, a = carve(a, 2, T)
        dbu, a = carve(a, NR, T)
        hs, a = carve(a, 2, NR, T)
        hc, a = carve(a, 2, NR, T)
        assert a <= REP_AT
        ga, a = carve(0, 2, T)
        h1, a = carve(a, TC, DM)
        xc3, a = carve(a, TC, DM)
        sq3, a = carve(a, TC, DM)
        xf, a = carve(a, TC, DM)
        xfT, a = carve(a, T, rows=DM + 1)
        lg, a = carve(a, TC, E)
        oh, a = carve(a, TC, E)
        mx, a = carve(a, TC)
        mx2, a = carve(a, TC)
        ohT, a = carve(a, T, rows=E)
        hid, a = carve(a, NBLK, T)
        fin, a = carve(a, TC, DM)
        ohTb = sb("ohTb", [E + 1, T], BF16)

        def conv_wT(d, k):
            return wT[:, 2 + 4 * d + k, :]

        def flat(ap):
            return ap.rearrange("p a b -> p (a b)")

        A = lambda n: ins["L0_attn_" + n]
        loads = []

        def load(dst, src):
            loads.append((dst, src))

        load(in_w, A("in_w").rearrange("(h c) j -> c h j", h=2))
        load(conv_w[:, 0, :], A("conv_w"))
        load(conv_b[:, 0:1], A("conv_b").rearrange("(c a) -> c a", a=1))
        for h in range(2):
            load(ln_g[DM * h:DM * h + DM], A("ln_g").rearrange("(c a) -> c a", a=1))
            load(ln_b[DM * h:DM * h + DM], A("ln_b").rearrange("(c a) -> c a", a=1))
        load(out_w, A("out_w"))
        for d, n in enumerate(DIRS):
            load(dir_w[:, d], A(n + "_in_w").rearrange("(h c) j -> c h j", h=2))
            load(conv_w[:, 1 + d, :], A(n + "_conv_w"))
            load(conv_b[:, 1 + d:2 + d], A(n + "_conv_b").rearrange("(c a) -> c a", a=1))
            load(xdt[:, d], A(n + "_xproj_w")[0:R, :])
            load(xbc[:, d], A(n + "_xproj_w")[R:R + 2 * NS, :])
            load(dt_w[:, d], A(n + "_dt_w"))
            load(dt_b[:, d:d + 1], A(n + "_dt_b").rearrange("(c a) -> c a", a=1))
            load(dskip[:, d:d + 1], A(n + "_D").rearrange("(c a) -> c a", a=1))
            load(dir_ow[:, d], A(n + "_out_w"))
            for m in range(4):
                load(alog[32 * m:32 * m + 32, d], A(n + "_Alog").rearrange("(q d) s -> d q s", d=32))
        F = lambda n: ins["L0_ffn_" + n]
        load(router_w, F("router_w"))
        load(router_wT[DM:DM + 1, :], F("router_b").rearrange("(a e) -> a e", a=1))
        load(w1[:], F("W1").rearrange("e d h -> d e h"))
        load(b1[:], F("b1").rearrange("e h -> (e h)").rearrange("(n p) -> p n", p=P))
        load(w2[:], F("W2").rearrange("e h d -> (e h) d").rearrange("(n p) d -> p n d", p=P))
        load(b2[:], F("b2"))

        block = ctx.enter_context(nc.Block())
        NLN = 2 * B

        PAIR = 2 * NQ * NR

        def bank(d, tile):
            return (NQ * NR * d + tile) % 3

        def bank_age(d, tile):
            at = NQ * NR * d + tile
            return next(n for n in range(1, PAIR) if (at - n) % PAIR % 3 == at % 3)

        @block.sync
        def _(sp):
            sp.dma_start(ids[:], x.rearrange("b (t p) -> (b t) p", p=P)).then_inc(sem("ids_in"), 16)
            with nc.allow_non_contiguous_dma(reason="b1 is 2 KB"):
                for dst, src in loads:
                    sp.dma_start(dst, src).then_inc(sem("weights_in"), 16)

            with sp.Fori(0, NCH) as n:
                for d in range(2):
                    sp.wait_ge(sem("bc_in_sbuf"), 2 * n + d + 1)
                    sp.dma_start(bc_dram[d, :, bass.ds(n * T, T)], bc_sb[:, d, :]) \
                      .then_inc(sem("bc_in_dram"), 16)

            def load_rep(i, d):
                for m in range(4):
                    src = bc_dram[d].rearrange("(k m) t -> m k t", m=4)[m]
                    src = src.unsqueeze(0).broadcast_to([32, 2 * NR, NTOK])[:, :, bass.ds(i * T, T)]
                    sp.dma_start(rep[32 * m:32 * m + 32, d].rearrange("p a b t -> p (a b) t"), src) \
                      .then_inc(sem(f"rep_in_{DIRS[d]}"), 16)

            sp.wait_ge(sem("bc_in_dram"), 16 * UNITS)
            sp.wait_ge(sem("setup_dve"), 1)
            for d in range(2):
                load_rep(0, d)
            with sp.Fori(1, NCH) as i:
                for d in range(2):
                    sp.wait_ge(sem("hc_ready"), NQ * 2 * i + NQ * (d - 1))
                    load_rep(i, d)

            with sp.Fori(0, NCH) as n:
                sp.wait_ge(sem("fin_ready"), n + 1)
                sp.dma_start(out.rearrange("b (t p) d -> p (b t) d", p=P)[:, bass.ds(n * TC, TC), :], fin) \
                  .then_inc(sem("out_done"), 16)
            sp.wait_ge(sem("out_done"), 16 * NCH)

        @block.gpsimd
        def _(pool):
            ch = Chain(pool, sem("pool_step"))

            def fill_where(view, pattern, base, fill):
                ch.step(pool.affine_select(out=view, in_=view, compare_op=ALU.not_equal, fill=fill,
                                           base=base, pattern=pattern, channel_multiplier=1))

            ch.step(pool.memset(ident[:], 0.0))
            ch.step(pool.memset(fold[:], 0.0))
            ch.step(pool.memset(pickf, 0.0))
            fill_where(ident[:], [[-1, P]], 0, 1.0)
            for m in range(4):
                fill_where(fold[:], [[-1, 32]], -32 * m, 1.0)
            fill_where(pickf.rearrange("p n (e h) -> p n e h", h=H),
                       [[-(P // H), NBLK], [-1, P // H], [0, H]], 0, BIG)
            ch.step(pool.memset(pickf[E:E + 1], -BIG))
            ch.step(pool.iota(ranki[:], pattern=[[-1, E]], base=E, channel_multiplier=0))
            ch.step(pool.memset(eps[:], EPS))
            pool.memset(lns[:], 0.0).then_inc(sem("consts"), 1)

            rows = table.rearrange("v (s d) -> (v s) d", d=DM)
            pool.wait_ge(sem("idx_ready"), 1)
            for t in range(TILES):
                pool.indirect_dma_start(
                    out=x0[:, t, :], out_offset=None, in_=rows,
                    in_offset=bass.IndirectOffsetOnAxis(ap=idx[:, t:t + 1], axis=0),
                ).then_inc(sem(f"gathered_{t // TB}"), 16)

            def by_c(i, d, q):
                unit = 2 * i + d
                done = NQ * unit + q
                pool.wait_ge(sem("scans"), NR * (done + 1))
                if q == 0:
                    pool.wait_ge(sem(f"rep_in_{DIRS[d]}"), 64 * (i + 1))
                pool.wait_ge(sem("summed"), done - 1)
                pool.tensor_tensor(flat(hc[:, q % 2]), flat(hs[:, q % 2]),
                                   rep[:, d, 1].rearrange("p a t -> p (a t)"), ALU.mult) \
                    .then_inc(sem("hc_ready"), 1)

            def unit_pair(i, first=False):
                for d in range(2):
                    for q in range(NQ):
                        if first and d == 0 and q < 2:
                            pool.wait_ge(sem("scans"), NR * (q + 1))
                            pool.wait_ge(sem("rep_in_f"), 64)
                            pool.tensor_tensor(flat(hc[:, q]), flat(hs[:, q]),
                                               rep[:, 0, 1].rearrange("p a t -> p (a t)"), ALU.mult) \
                                .then_inc(sem("hc_ready"), 1)
                        else:
                            by_c(i, d, q)

            unit_pair(0, first=True)
            with pool.Fori(1, NCH) as i:
                unit_pair(i)

        @block.tensor
        def _(pe):
            pe.wait_ge(sem("consts"), 1)
            pe.wait_ge(sem("ids_clamped"), 1)
            pe.transpose(ps[:, 6, 0:TILES], idx_f, ident[0:TILES, 0:TILES]).then_inc(sem("idx_ps"), 1)

            pe.wait_ge(sem("weights_in"), 16 * len(loads))
            pe.wait_ge(sem("taps_ready"), 1)

            def turn(slot, src, cols=None, at=0):
                k, m = src.shape[0], src.shape[1]
                return pe.transpose(ps[0:m, slot // 4, (slot % 4) * P + at:(slot % 4) * P + at + k],
                                    src, ident[0:k, 0:k])

            for s in range(2):
                turn(s, flat(taps[:, s]))
            for d in range(2):
                for k in range(4):
                    turn(2 + 4 * d + k, dir_taps[:, d, k])
            for d in range(2):
                turn(10 + d, dir_w[:, d, 1])
                turn(12 + d, dir_ow[:, d])
                turn(14, out_w[:, P * d:P * d + P], at=DM * d)
                turn(15, xbc[:, d], at=2 * NS * d)
            turn(16, in_w[:, 1])
            turn(17, router_w)
            for d in range(2):
                mm = turn(18 + d, dt_w[:, d])
            mm.then_inc(sem("wT_ps"), 1)
            pe.wait_ge(sem("wT_ready"), 1)
            for d in range(2):
                mm = pe.matmul(ps[:, 5, P * d:P * d + P], xdt[:, d], dt_wT[:, d], start=True, stop=True)
            mm.then_inc(sem("dtproj_ps"), 1)
            pe.wait_ge(sem("wT_ready"), 2)

            for b in range(B):
                pe.wait_ge(sem("u2_ready"), b + 1)
                for c2 in range(CB // 2):
                    for k in range(2):
                        n = CB * b + 2 * c2 + k
                        if n:
                            pe.wait_ge(sem("uT_act"), n)
                            pe.wait_ge(sem("uT_dve"), n)
                        for t in range(TC):
                            tr = pe.transpose(
                                ps[:, k, t * P:t * P + P],
                                flat(u2d[:, TC * (2 * c2 + k) + t]),
                                ident[:])
                        tr.then_inc(sem("turned"), 1)
                        pe.wait_ge(sem("uT_act"), n + 1)
                        pe.wait_ge(sem("uT_dve"), n + 1)
                        if n:
                            pe.wait_ge(sem("act_r_ready"), n)
                            pe.wait_ge(sem("gate_ready"), n)
                        for s in range(2):
                            mm = pe.matmul(ps[:, 2 + k, :], wT[:, s, :],
                                           uT[:, b, bass.ds((2 * c2 + k) * T + 3 - 2 * s, T)],
                                           start=(s == 0), stop=(s == 1))
                        mm.then_inc(sem("x_ps"), 1)
                        pe.matmul(ps[:, 4 + k, :], gate_wT[:], uT[0:DM, b, bass.ds((2 * c2 + k) * T + 3, T)],
                                  start=True, stop=True).then_inc(sem("gate_ps"), 1)

            pe.wait_ge(sem("act_ready"), NCH)
            pe.wait_ge(sem("act_r_ready"), NCH)
            pe.wait_ge(sem("act_r_edges"), 1)
            pe.wait_ge(sem("gate_ready"), NCH)
            for b in range(B):
                with pe.Fori(0, CB) as c:
                    n = CB * b + c
                    for d in range(2):
                        src = (act, act_r)[d][:, b, :]
                        pe.wait_ge(sem("xs_ready"), 2 * n + d)
                        pe.wait_ge(sem("z_ready"), 2 * n + d)
                        for k in range(4):
                            mm = pe.matmul(ps[:, 6 + d, :], conv_wT(d, k), src[:, bass.ds(c * T + k, T)],
                                           start=(k == 0), stop=(k == 3))
                        mm.then_inc(sem("xs_ps"), 1)
                        pe.matmul(ps[:, d, :], wT[:, 10 + d, :], src[:, bass.ds(c * T + 3, T)],
                                  start=True, stop=True).then_inc(sem("z_ps"), 1)
                    for d in range(2):
                        pe.wait_ge(sem("xs_ready"), 2 * n + d + 1)
                        pe.wait_ge(sem("bc_in_sbuf"), 2 * n + d)
                        pe.matmul(ps[0:2 * NS, 2 + d, :], wT[:, 15, 2 * NS * d:2 * NS * d + 2 * NS],
                                  xs[:, d, bass.ds(n * T, T)], start=True, stop=True) \
                          .then_inc(sem("bc_ps"), 1)

            def pre(i, d, wait_free=True):
                if wait_free:
                    pe.wait_ge(sem("softplus_w"), 2 * i + d)
                pe.matmul(ps[:, 2, :], dtproj[:, d, :], xs[:, d, bass.ds(i * T, T)], start=True, stop=True) \
                  .then_inc(sem("pre_ps"), 1)

            def reps(i, d, q):
                done = NQ * (2 * i + d) + q
                if q == 0:
                    pe.wait_ge(sem("dt_ready"), 2 * i + d + 1)
                pe.wait_ge(sem("decay_ready"), NR * done)
                pe.matmul(ps[:, 0, :], spread[:, q, :], dt[:, d], start=True, stop=True) \
                  .then_inc(sem("dt_spread"), 1)
                if q == 0:
                    pe.wait_ge(sem("du_ready"), 2 * i + d + 1)
                pe.wait_ge(sem("dbu_ready"), done)
                pe.matmul(ps[:, 1, :], spread[:, q, :], du[:, d], start=True, stop=True) \
                  .then_inc(sem("du_spread"), 1)

            def nsum(i, d, q):
                if q == 0:
                    if not (isinstance(i, int) and i == 0):
                        pe.wait_ge(sem("yz_ready"), 2 * i + d - 1)
                    pe.matmul(ps[:, 6 + d, :], skip[:, d, :], xs[:, d, bass.ds(i * T, T)],
                              start=True, stop=False, skip_group_check=True)
                pe.wait_ge(sem("hc_ready"), NQ * (2 * i + d) + q + 1)
                for r in range(NR):
                    mm = pe.matmul(ps[32 * q:32 * q + 32, 6 + d, :], fold[:], hc[:, q % 2, r],
                                   start=False, stop=(r == NR - 1), skip_group_check=True)
                mm.then_inc(sem("summed"), 1)

            def unit(i, d, first=False, last=False):
                for q in range(NQ):
                    reps(i, d, q)
                    if q >= 2:
                        nsum(i, d, q - 2)
                    elif not first:
                        nsum(i if d else i - 1, 1 - d, q + 2)
                    if q == 1 and not last:
                        pre(i + d, 1 - d)

            pe.wait_ge(sem("bc_in_sbuf"), UNITS)
            pe.wait_ge(sem("z_ready"), UNITS)
            pe.wait_ge(sem("setup_dve"), 1)
            pre(0, 0, wait_free=False)
            unit(0, 0, first=True)
            unit(0, 1)
            with pe.Fori(1, NCH - 1) as i:
                unit(i, 0)
                unit(i, 1)
            unit(NCH - 1, 0)
            unit(NCH - 1, 1, last=True)
            nsum(NCH - 1, 1, 2)
            nsum(NCH - 1, 1, 3)

            pe.wait_ge(sem("yz_ready"), UNITS)
            for b in range(B):
                with pe.Fori(0, CB) as c:
                    n = CB * b + c
                    pe.wait_ge(sem("gated"), 2 * n)
                    for d in range(2):
                        at = b * L + (c * T if d == 0 else (CB - 1) * T - c * T)
                        pe.matmul(ps[:, d, :], wT[:, 12 + d, :], z[:, d, bass.ds(at, T)],
                                  start=True, stop=True).then_inc(sem("dir_out"), 1)
                    pe.wait_ge(sem("h1_sum"), n)
                    pe.wait_ge(sem("gated"), 2 * n + 2)
                    for t in range(TC):
                        for d in range(2):
                            mm = pe.matmul(ps[:, 2, t * DM:t * DM + DM], ga[:, d, t * P:t * P + P],
                                           wT[:, 14, DM * d:DM * d + DM], start=(d == 0), stop=(d == 1))
                    mm.then_inc(sem("attn_ps"), 1)
                    pe.wait_ge(sem("xf_ready"), n + 1)
                    for h in range(TC // 2):
                        tr = pe.transpose(ps[:, 3, h * P:h * P + P], flat(xf[:, 2 * h:2 * h + 2]), ident[:])
                    tr.then_inc(sem("xfT_ps"), 1)
                    pe.wait_ge(sem("xfT_ready"), 2 * n + 2)
                    for t in range(TC):
                        mm = pe.matmul(ps[:, 3, t * E:t * E + E], xfT[:, t * P:t * P + P], router_wT[:],
                                       start=True, stop=True)
                    mm.then_inc(sem("logits_ps"), 1)
                    pe.wait_ge(sem("choice_ready"), n + 1)
                    for t in range(TC):
                        tr = pe.transpose(ps[0:E, 4, t * P:t * P + P], oh[:, t], ident[:])
                    tr.then_inc(sem("choice_ps"), 1)
                    pe.wait_ge(sem("choiceT_bf16"), n + 1)
                    for k in range(NBLK):
                        pe.wait_ge(sem("hidden"), NBLK * n + k - 1 if k else NBLK * n)
                        pe.matmul(ps[:, 5 + k % 2, :], pick[:, k, :], ohTb[:], start=True, stop=False)
                        pe.matmul(ps[:, 5 + k % 2, :], w1[:, 8 * k:8 * k + 8, :].rearrange("p e h -> p (e h)"),
                                  xfT[0:DM, :], start=False, stop=True).then_inc(sem("hidden_ps"), 1)
                    pe.wait_ge(sem("hidden"), NBLK * n + NBLK)
                    pe.wait_ge(sem("fin_ready"), n)
                    for t in range(TC):
                        for k in range(NBLK):
                            pe.matmul(ps[:, 7, t * DM:t * DM + DM], hid[:, k, t * P:t * P + P], w2[:, k, :],
                                      start=(k == 0), stop=False)
                        mm = pe.matmul(ps[:, 7, t * DM:t * DM + DM], ohT[:, t * P:t * P + P], b2[:],
                                       start=False, stop=True)
                    mm.then_inc(sem("moe_ps"), 1)

        @block.scalar
        def _(act_e):
            ch = Chain(act_e, sem("act_step"))

            def ln_part(ordinal, xc, sq, width):
                act_e.wait_ge(sem("ln_centred"), ordinal)
                act_e.activation(sq, xc, ACT.Square).then_inc(sem("ln_squares"), 1)
                act_e.wait_ge(sem("ln_sumsq"), ordinal)
                act_e.activation(lns[:, 2, 0:width], lns[:, 1, 0:width], ACT.Ln, scale=1.0 / DM,
                                 bias=eps[:, 0:1]).then_inc(sem("ln_log"), 1)
                act_e.wait_ge(sem("ln_log"), ordinal)
                act_e.activation(lns[:, 3, 0:width], lns[:, 2, 0:width], ACT.Exp, scale=-0.5) \
                     .then_inc(sem("ln_rsqrt"), 1)

            act_e.wait_ge(sem("weights_in"), 16 * len(loads))
            for m in range(4):
                rows = slice(32 * m, 32 * m + 32)
                act_e.activation(negA[rows].rearrange("p a b c -> p (a b) c"),
                                 alog[rows].rearrange("p a b (r m) -> p (a b) r m", m=4)[:, :, :, m],
                                 ACT.Exp).then_inc(sem("expA"), 1)
            act_e.wait_ge(sem("consts"), 1)

            for b in range(B):
                for k in range(2):
                    ln_part(2 * b + k + 1, flat(xc), flat(sq), TB)
                if b == 0:
                    act_e.wait_ge(sem("setup_dve"), 1)
                with act_e.Fori(0, CB // 2) as c2:
                    for k in range(2):
                        n = CB * b + 2 * c2 + k
                        at = (2 * c2 + k) * T + 3
                        act_e.wait_ge(sem("turned"), n + 1)
                        act_e.activation(uT[0:DM, b, bass.ds(at, T)], ps[0:DM, k, :], ACT.Identity,
                                         scale=ln_g[0:DM, 0:1], bias=ln_b[0:DM, 0:1]) \
                             .then_inc(sem("uT_act"), 1)
                        act_e.wait_ge(sem("x_ps"), n + 1)
                        act_e.activation(act[:, b, bass.ds(at, T)], ps[:, 2 + k, :], ACT.Silu,
                                         bias=conv_b[:, 0:1]).then_inc(sem("act_ready"), 1)
                        act_e.activation(act_r[:, b, bass.ds(L - T + 6 - at, T)], ps[:, 2 + k, REV], ACT.Silu,
                                         bias=conv_b[:, 0:1]).then_inc(sem("act_r_ready"), 1)
                        act_e.wait_ge(sem("gate_ps"), n + 1)
                        act_e.activation(gate[:, bass.ds(n * T, T)], ps[:, 4 + k, :], ACT.Silu) \
                             .then_inc(sem("gate_ready"), 1)

            with act_e.Fori(0, NCH) as n:
                for d in range(2):
                    act_e.wait_ge(sem("xs_ps"), 2 * n + d + 1)
                    act_e.activation(xs[:, d, bass.ds(n * T, T)], ps[:, 6 + d, :], ACT.Silu,
                                     bias=conv_b[:, 1 + d:2 + d]).then_inc(sem("xs_ready"), 1)
                    act_e.wait_ge(sem("z_ps"), 2 * n + d + 1)
                    act_e.activation(z[:, d, bass.ds(n * T, T)], ps[:, d, :], ACT.Silu) \
                         .then_inc(sem("z_ready"), 1)

            def softplus(i, d, first=False):
                unit = 2 * i + d
                act_e.wait_ge(sem("pre_ps"), unit + 1)
                if not first:
                    act_e.wait_ge(sem("dt_ready"), unit)
                act_e.activation(v_, ps[:, 2, :], ACT.Identity, bias=dt_b[:, d:d + 1]) \
                     .then_inc(sem("softplus_v"), 1)
                act_e.activation(w_, ps[:, 2, :], ACT.Abs, bias=dt_b[:, d:d + 1]).then_inc(sem("softplus_a"), 1)
                act_e.wait_ge(sem("softplus_a"), unit + 1)
                act_e.activation(e_, w_, ACT.Exp, scale=-1.0).then_inc(sem("softplus_e"), 1)
                act_e.wait_ge(sem("softplus_e"), unit + 1)
                act_e.activation(w_, e_, ACT.Identity, bias=1.0).then_inc(sem("softplus_w"), 1)
                act_e.wait_ge(sem("softplus_w"), unit + 1)
                act_e.activation(l_, w_, ACT.Ln).then_inc(sem("softplus_l"), 1)

            def decays(i, d, q, first=False):
                done = NQ * (2 * i + d) + q
                act_e.wait_ge(sem("dt_spread"), done + 1)
                for r in range(NR):
                    tile = NR * q + r
                    if not (first and tile < 3):
                        act_e.wait_ge(sem("scans"), NR * done + r + 1 - bank_age(d, tile))
                    act_e.activation(ps[:, 3 + bank(d, tile), :], ps[:, 0, :], ACT.Exp,
                                     scale=negA[:, d, q, r:r + 1]).then_inc(sem("decay_ready"), 1)

            def unit_act(i, d, first=False, last=False):
                for q in range(NQ):
                    decays(i, d, q, first)
                    if q == 1 and not last:
                        softplus(i + d, 1 - d)

            softplus(0, 0, first=True)
            act_e.wait_ge(sem("setup_dve"), 1)
            unit_act(0, 0, first=True)
            unit_act(0, 1)
            with act_e.Fori(1, NCH - 1) as i:
                unit_act(i, 0)
                unit_act(i, 1)
            unit_act(NCH - 1, 0)
            unit_act(NCH - 1, 1, last=True)

            with act_e.Fori(0, NCH) as n:
                ln_part(NLN + n + 1, flat(xc3), flat(sq3), TC)
                act_e.wait_ge(sem("xfT_ps"), n + 1)
                for h in range(2):
                    act_e.activation(
                        xfT[0:DM, :].rearrange("p (g h t) -> p g h t", h=2, t=P)[:, :, h],
                        ps[DM * h:DM * h + DM, 3, 0:T // 2].rearrange("p (g t) -> p g t", t=P),
                        ACT.Copy).then_inc(sem("xfT_ready"), 1)
                act_e.wait_ge(sem("choiceT"), n + 1)
                act_e.activation(ohTb[0:E, :], ohT, ACT.Copy).then_inc(sem("choiceT_bf16"), 1)
                for k in range(NBLK):
                    act_e.wait_ge(sem("hidden_ps"), NBLK * n + k + 1)
                    act_e.activation(hid[:, k, :], ps[:, 5 + k % 2, :], ACT.Relu, bias=b1[:, k:k + 1]) \
                         .then_inc(sem("hidden"), 1)

        @block.vector
        def _(dve):
            ch = Chain(dve, sem("dve_step"))

            dve.wait_ge(sem("ids_in"), 16)
            dve.wait_ge(sem("consts"), 1)
            ch.step(dve.tensor_copy(idx_f, ids[:]))
            ch.step(dve.tensor_scalar(idx_g, idx_f, 0.0, float(V), ALU.is_lt, ALU.mult))
            ch.step(dve.tensor_tensor(idx_g, idx_g, idx_f, ALU.add))
            ch.step(dve.tensor_scalar(idx_g, idx_g, 0.0, float(V - 1), ALU.max, ALU.min))
            dve.tensor_scalar(idx_f, idx_g, float(HID // DM), float(SLICE), ALU.mult, ALU.add) \
               .then_inc(sem("ids_clamped"), 1)
            dve.wait_ge(sem("idx_ps"), 1)
            dve.tensor_copy(idx[:], ps[:, 6, 0:TILES]).then_inc(sem("idx_ready"), 1)

            dve.wait_ge(sem("weights_in"), 16 * len(loads))
            for k in range(4):
                ch.mark(dve.tensor_scalar(taps[:, (3 - k) // 2, (3 - k) % 2, :], in_w[:, 0, :],
                                          conv_w[:, 0, k:k + 1], None, ALU.mult))
                for d in range(2):
                    ch.mark(dve.tensor_scalar(dir_taps[:, d, k, :], dir_w[:, d, 0, :],
                                              conv_w[:, 1 + d, k:k + 1], None, ALU.mult))
            ch.wait()
            dve.tensor_copy(spread[:].rearrange("p q (n d) -> p q n d", d=32),
                            ident[:].rearrange("p (q d) -> p q d", d=32).unsqueeze(2)
                            .broadcast_to([P, NQ, 4, 32])).then_inc(sem("taps_ready"), 1)
            for d in range(2):
                ch.mark(dve.tensor_scalar(skip[:, d, :], ident[:], dskip[:, d:d + 1], None, ALU.mult))
            dve.wait_ge(sem("expA"), 4)
            ch.mark(dve.tensor_scalar(negA[:].rearrange("p a b c -> p (a b c)"),
                                      negA[:].rearrange("p a b c -> p (a b c)"), -1.0, None, ALU.mult))
            ch.mark(dve.tensor_copy(rank[:], ranki[:]))
            ch.mark(dve.tensor_copy(pick[:], pickf))
            dve.wait_ge(sem("wT_ps"), 1)
            for k in range(3):
                ch.mark(dve.tensor_copy(wT[:, 4 * k:4 * k + 4, :].rearrange("p a b -> p (a b)"), ps[:, k, :]))
            ch.mark(dve.tensor_copy(wT[:, 12:15, :].rearrange("p a b -> p (a b)"), ps[:, 3, 0:3 * P]))
            ch.mark(dve.tensor_copy(wT[:, 15, 0:4 * NS], ps[:, 3, 3 * P:3 * P + 4 * NS]))
            ch.mark(dve.tensor_copy(gate_wT[:], ps[0:DM, 4, 0:P]))
            ch.mark(dve.tensor_copy(router_wT[0:DM, :], ps[0:DM, 4, P:P + E]))
            ch.wait()
            dve.tensor_copy(dt_wT[:].rearrange("p a b -> p (a b)"), ps[0:R, 4, 2 * P:4 * P]) \
               .then_inc(sem("wT_ready"), 1)
            dve.wait_ge(sem("dtproj_ps"), 1)
            dve.tensor_copy(dtproj[:].rearrange("p a b -> p (a b)"), ps[:, 5, 0:2 * P]) \
               .then_inc(sem("wT_ready"), 1)
            ch.mark(dve.memset(uT[:, :, 0:4], 0.0))
            ch.mark(dve.memset(act[:, :, 0:3], 0.0))
            ch.mark(dve.memset(act[:, :, L + 3:L + 6], 0.0))
            ch.mark(dve.memset(carry[:].rearrange("p a b c -> p (a b c)"), 0.0))
            ch.wait()
            dve.wait_ge(sem("wT_ready"), 2)
            dve.memset(ohTb[E:E + 1, :], 1.0).then_inc(sem("setup_dve"), 1)
            ch.mark(dve.memset(act_r[:, :, 0:3], 0.0))
            ch.wait()
            dve.memset(act_r[:, :, L + 3:L + 6], 0.0).then_inc(sem("act_r_edges"), 1)

            def layernorm(ordinal, src, xc, sq, outs, width):
                s = lambda k: lns[:, k, 0:width]
                wide = lambda k: s(k).unsqueeze(2).broadcast_to([P, width, DM])
                ch.step(dve.tensor_reduce(s(0), src, AX, ALU.add))
                ch.step(dve.tensor_scalar(s(0), s(0), 1.0 / DM, None, ALU.mult))
                dve.tensor_tensor(xc, src, wide(0), ALU.subtract).then_inc(sem("ln_centred"), 1)
                dve.wait_ge(sem("ln_squares"), ordinal)
                dve.tensor_reduce(s(1), sq, AX, ALU.add).then_inc(sem("ln_sumsq"), 1)
                dve.wait_ge(sem("ln_sumsq"), ordinal)
                ch.mark(dve.tensor_scalar(s(4), s(1), 1.0 / DM, EPS, ALU.mult, ALU.add))
                dve.wait_ge(sem("ln_rsqrt"), ordinal)
                ch.step(dve.tensor_tensor(s(5), s(3), s(3), ALU.mult))
                ch.step(dve.tensor_tensor(s(5), s(5), s(4), ALU.mult))
                ch.step(dve.tensor_scalar(s(5), s(5), -0.5, 1.5, ALU.mult, ALU.add))
                ch.step(dve.tensor_tensor(s(6), s(5), s(3), ALU.mult))
                for o in outs[:-1]:
                    ch.mark(dve.tensor_tensor(o, xc, wide(6), ALU.mult))
                return dve.tensor_tensor(outs[-1], xc, wide(6), ALU.mult)
            LN_STEPS = 7

            for b in range(B):
                dve.wait_ge(sem(f"gathered_{b}"), 16 * TB)
                ub = u[:, TB * b:TB * b + TB, :]
                ch.step(layernorm(2 * b + 1, x0[:, TB * b:TB * b + TB, :], xc, sq, [ub], TB))
                if b:
                    dve.wait_ge(sem("turned"), CB * b)
                last = layernorm(2 * b + 2, ub, xc, sq, [u2d[:, :, 0, :], u2d[:, :, 1, :]], TB)
                ch.wait()
                last.then_inc(sem("u2_ready"), 1)
                with dve.Fori(0, CB // 2) as c2:
                    for k in range(2):
                        n = CB * b + 2 * c2 + k
                        dve.wait_ge(sem("turned"), n + 1)
                        dve.tensor_scalar(uT[DM:P, b, bass.ds((2 * c2 + k) * T + 4, T)], ps[DM:P, k, :],
                                          ln_g[DM:P, 0:1], ln_b[DM:P, 0:1], ALU.mult, ALU.add) \
                           .then_inc(sem("uT_dve"), 1)

            with dve.Fori(0, NCH) as n:
                for d in range(2):
                    dve.wait_ge(sem("bc_ps"), 2 * n + d + 1)
                    dve.wait_ge(sem("bc_in_dram"), 16 * (2 * n))
                    dve.tensor_copy(bc_sb[:, d, :], ps[0:2 * NS, 2 + d, :]).then_inc(sem("bc_in_sbuf"), 1)

            def softplus(i, d):
                unit = 2 * i + d
                dve.wait_ge(sem("softplus_l"), unit + 1)
                dve.scalar_tensor_tensor(e_, w_, -1.0, e_, ALU.add, ALU.subtract).then_inc(sem("sp_c"), 1)
                dve.wait_ge(sem("sp_c"), unit + 1)
                dve.tensor_tensor(l_, l_, e_, ALU.subtract).then_inc(sem("sp_log1p"), 1)
                dve.wait_ge(sem("sp_log1p"), unit + 1)
                dve.scalar_tensor_tensor(dt[:, d], v_, 0.0, l_, ALU.max, ALU.add).then_inc(sem("dt_ready"), 1)
                dve.wait_ge(sem("dt_ready"), unit + 1)
                dve.tensor_tensor(du[:, d], dt[:, d], xs[:, d, bass.ds(i * T, T)], ALU.mult) \
                   .then_inc(sem("du_ready"), 1)

            def group(i, d, q, first=False, reset=False):
                done = NQ * (2 * i + d) + q
                dve.wait_ge(sem("du_spread"), done + 1)
                if q == 0:
                    dve.wait_ge(sem(f"rep_in_{DIRS[d]}"), 64 * (i + 1))
                dve.tensor_tensor(dbu, ps[:, 1, :].unsqueeze(1).broadcast_to([P, NR, T]), rep[:, d, 0],
                                  ALU.mult).then_inc(sem("dbu_ready"), 1)
                dve.wait_ge(sem("dbu_ready"), done + 1)
                if not (first and q < 2):
                    dve.wait_ge(sem("hc_ready"), done - 1)
                for r in range(NR):
                    dve.wait_ge(sem("decay_ready"), NR * done + r + 1)
                    dve.tensor_tensor_scan(hs[:, q % 2, r], ps[:, 3 + bank(d, NR * q + r), :], dbu[:, r],
                                           carry[:, d, q, r:r + 1], ALU.mult, ALU.add) \
                       .then_inc(sem("scans"), 1)
                dve.wait_ge(sem("scans"), NR * done + NR)
                if reset:
                    ch.step(dve.memset(carry[:, d, q], 0.0))
                else:
                    ch.step(dve.tensor_copy(carry[:, d, q], hs[:, q % 2, :, T - 1]))

            def y_by_z(i, d):
                unit = 2 * i + d
                dve.wait_ge(sem("summed"), NQ * unit + NQ)
                zc = z[:, d, bass.ds(i * T, T)]
                dve.tensor_tensor(zc, ps[:, 6 + d, :], zc, ALU.mult).then_inc(sem("yz_ready"), 1)

            def unit_dve(i, d, first=False, last=False, reset=False):
                for q in range(NQ):
                    group(i, d, q, first, reset)
                    if q == 2 and not last:
                        softplus(i + d, 1 - d)
                    if q == 2 and not first:
                        y_by_z(i if d else i - 1, 1 - d)

            @marks(2 * NQ)
            def pair(i):
                unit_dve(i, 0)
                unit_dve(i, 1)

            softplus(0, 0)
            unit_dve(0, 0, first=True)
            unit_dve(0, 1)
            for b in range(B):
                if b == 0:
                    ch.loop(1, CB - 1, pair)
                    for d in range(2):
                        unit_dve(CB - 1, d, reset=True)
                else:
                    ch.loop(CB * b, CB * b + CB - 1, pair)
                    for d in range(2):
                        unit_dve(CB * b + CB - 1, d, last=(d == 1))
            y_by_z(NCH - 1, 1)

            dve.wait_ge(sem("summed"), NQ * UNITS)
            ch.step(dve.memset(xfT[DM:DM + 1, :], 1.0))

            @marks(2 + LN_STEPS + 5)
            def chunk(n):
                for d in range(2):
                    dve.wait_ge(sem("dir_out"), 2 * n + d + 1)
                    if d == 0:
                        dve.wait_ge(sem("attn_ps"), n)
                    dve.tensor_tensor(ga[:, d], ps[:, 0, :] if d == 0 else ps[:, 1, REV], gate[:, bass.ds(n * T, T)], ALU.mult) \
                       .then_inc(sem("gated"), 1)
                dve.wait_ge(sem("attn_ps"), n + 1)
                dve.tensor_tensor(flat(h1), ps[:, 2, 0:TC * DM], flat(u[:, bass.ds(n * TC, TC), :]), ALU.add) \
                   .then_inc(sem("h1_sum"), 1)
                dve.wait_ge(sem("h1_sum"), n + 1)
                ch.step(dve.tensor_tensor(flat(h1), flat(h1), flat(x0[:, bass.ds(n * TC, TC), :]), ALU.add))
                ch.mark_last = layernorm(NLN + n + 1, h1, xc3, sq3, [xf], TC)
                ch.mark_last.then_inc(sem("xf_ready"), 1)
                dve.wait_ge(sem("logits_ps"), n + 1)
                ch.step(dve.tensor_copy(flat(lg), ps[:, 3, 0:TC * E]))
                ch.step(dve.tensor_reduce(mx, lg, AX, ALU.max))
                ch.step(dve.tensor_tensor(lg, lg, mx.unsqueeze(2).broadcast_to([P, TC, E]), ALU.is_equal))
                ch.step(dve.tensor_tensor(lg, lg, rank[:].unsqueeze(1).broadcast_to([P, TC, E]), ALU.mult))
                ch.step(dve.tensor_reduce(mx2, lg, AX, ALU.max))
                ch.step(dve.memset(mx, 0.0))
                dve.tensor_tensor(oh, lg, mx2.unsqueeze(2).broadcast_to([P, TC, E]), ALU.is_equal) \
                   .then_inc(sem("choice_ready"), 1)
                dve.wait_ge(sem("choice_ps"), n + 1)
                dve.tensor_copy(ohT, ps[0:E, 4, :]).then_inc(sem("choiceT"), 1)
                dve.wait_ge(sem("moe_ps"), n + 1)
                dve.wait_ge(sem("out_done"), 16 * n)
                dve.scalar_tensor_tensor(flat(fin), ps[:, 7, 0:TC * DM], 0.0, flat(h1), ALU.max, ALU.add) \
                   .then_inc(sem("fin_ready"), 1)

            ch.loop(0, NCH, chunk)


_INS = ["x", "L0_tok_ple_table"] + ["L0_attn_" + n for n in (
    "ln_g", "ln_b", "in_w", "conv_w", "conv_b", "out_w")] + [
    f"L0_attn_{d}_{n}" for d in "fb" for n in (
        "in_w", "conv_w", "conv_b", "xproj_w", "dt_w", "dt_b", "Alog", "D", "out_w")] + [
    "L0_ffn_" + n for n in ("router_w", "router_b", "W1", "b1", "W2", "b2")]


def kernel(**inputs):
    import concourse.bacc as _bacc
    from concourse.bass_utils import run_bass_kernel_spmd as _run

    nc = _bacc.Bacc("TRN2", target_bir_lowering=False, num_devices=1)
    arrays, aps = {}, {}
    for name in _INS:
        a = np.ascontiguousarray(inputs[name])
        arrays[f"in_{name}"] = a
        aps[name] = nc.dram_tensor(f"in_{name}", a.shape, mybir.dt.from_np(a.dtype), kind="ExternalInput").ap()
    B, L = inputs["x"].shape
    out = nc.dram_tensor("out_h", (B, L, inputs["L0_attn_ln_g"].shape[0]), F32, kind="ExternalOutput").ap()
    build(nc, aps, out)
    r = _run(nc, [arrays], core_ids=[0])
    return r.results[0]["out_h"]
```

```python
from contextlib import ExitStack

import numpy as np

import concourse.bass as bass
from concourse import mybir
from concourse.alu_op_type import AluOpType as ALU

ACT = mybir.ActivationFunctionType
F32 = mybir.dt.float32
BF16 = mybir.dt.bfloat16
I32 = mybir.dt.int32
AX = mybir.AxisListType.X

P = 128
T = 512
NQ = 4
NR = 4
BIG = float(2.0 ** 120)
EPS = 1e-5
REV = slice(None, None, -1)


class Chain:

    def __init__(self, eng, sem):
        self.eng, self.sem, self.base, self.k = eng, sem, 0, 0

    def mark(self, ins):
        ins.then_inc(self.sem, 1)
        self.k += 1

    def wait(self):
        self.eng.wait_ge(self.sem, self.base + self.k)

    def step(self, ins):
        self.mark(ins)
        self.wait()

    def loop(self, start, end, body, per):
        base, k0 = self.base, self.k
        with self.eng.Fori(start, end) as i:
            self.base, self.k = base + k0 + (i - start) * per, 0
            body(i)
            assert self.k == per, self.k
        self.base, self.k = base, k0 + (end - start) * per


def build(nc, ins, out):
    x, table = ins["x"], ins["L0_tok_ple_table"]
    B, L = x.shape
    V, HID = table.shape
    DM = ins["L0_attn_ln_g"].shape[0]
    DH = ins["L0_attn_conv_w"].shape[0]
    NS = ins["L0_attn_f_Alog"].shape[1]
    R = ins["L0_attn_f_dt_w"].shape[1]
    E, _, H = ins["L0_ffn_W1"].shape
    SLICE = 3
    NTOK = B * L
    TILES = NTOK // P
    TB = TILES // B
    TC = T // P
    NCH = NTOK // T
    CB = L // T
    NBLK = E * H // P
    UNITS = 2 * NCH
    ARENA = 88 * 256
    DIRS = ("f", "b")
    assert DH == P and NQ * 32 == DH and NR * 4 == NS and 2 * DM == P

    with ExitStack() as ctx:
        def sb(name, shape, dt=F32):
            return ctx.enter_context(nc.sbuf_tensor(name, shape, dt))

        sems = {}

        def sem(name):
            if name not in sems:
                sems[name] = ctx.enter_context(nc.semaphore(name))
            return sems[name]

        ps = ctx.enter_context(nc.psum_tensor("ps", [P, 8, T], F32))
        bc_dram = nc.dram_tensor("bc_dram", (2, 2 * NS, NTOK), F32, kind="Internal").ap()

        ident = sb("ident", [P, P])
        spread = sb("spread", [P, NQ, P])
        fold = sb("fold", [P, 32])
        wT = sb("wT", [P, 16, P])
        gate_wT = sb("gate_wT", [DM, P])
        router_wT = sb("router_wT", [DM + 1, E])
        dt_wT = sb("dt_wT", [R, 2, P])
        dtproj = sb("dtproj", [P, 2, P])
        skip = sb("skip", [P, 2, P])
        negA = sb("negA", [P, 2, NQ, NR])
        dt_b = sb("dt_b", [P, 2])
        conv_b = sb("conv_b", [P, 3])
        ln_g = sb("ln_g", [P, 1])
        ln_b = sb("ln_b", [P, 1])
        eps = sb("eps", [P, 1])
        w1 = sb("w1", [DM, E, H])
        b1 = sb("b1", [P, NBLK])
        w2 = sb("w2", [P, NBLK, DM])
        b2 = sb("b2", [E, DM])
        pick = sb("pick", [E + 1, NBLK, P], BF16)
        rank = sb("rank", [P, E])
        carry = sb("carry", [P, 2, NQ, NR])
        lns = sb("lns", [P, 8, TB])
        x0 = sb("x0", [P, TILES, DM])
        gate = sb("gate", [P, NTOK])
        PADW = L + 3
        xs = sb("xs", [P, B, 2, PADW])
        z = sb("z", [P, 2, NTOK])
        ids = sb("ids", [TILES, P], I32)
        idx = sb("idx", [P, TILES], I32)
        ranki = sb("ranki", [P, E], I32)
        ohTb = sb("ohTb", [E + 1, T], BF16)
        arena = sb("arena", [P, ARENA])

        def carve(of, at, *shape, rows=P):
            n = int(np.prod(shape))
            v = of[0:rows, at:at + n]
            if len(shape) > 1:
                names = "abcd"[:len(shape)]
                v = v.rearrange(f"p ({' '.join(names)}) -> p {' '.join(names)}",
                                **{k: s for k, s in zip(names, shape)})
            return v, at + n

        uT, a = carve(arena, 0, B, L + 4)
        u2d, a = carve(arena, a, TB, 2, DM)
        u, a = carve(arena, a, TB, DM)
        xc, a = carve(arena, a, TB, DM)
        sq, a = carve(arena, a, TB, DM)
        in_w, a = carve(arena, a, 2, DM)
        conv_w, a = carve(arena, a, 3, 4)
        dir_w, a = carve(arena, a, 2, 2, P)
        taps, a = carve(arena, a, 2, 2, DM)
        dir_taps, a = carve(arena, a, 2, 4, P)
        xbc, a = carve(arena, a, 2, P, rows=2 * NS)
        xdt, a = carve(arena, a, 2, P, rows=R)
        dt_w, a = carve(arena, a, 2, R)
        dskip, a = carve(arena, a, 2)
        dir_ow, a = carve(arena, a, 2, P)
        out_w, a = carve(arena, a, 4 * DM, rows=DM)
        router_w, a = carve(arena, a, DM, rows=E)
        alog, a = carve(arena, a, 2, NQ, NS)
        pickf, a = carve(arena, a, NBLK, P, rows=E + 1)
        idx_f, a = carve(arena, a, P, rows=TILES)
        idx_g, a = carve(arena, a, P, rows=TILES)
        assert a <= ARENA
        v_, a = carve(arena, 0, T)
        e_, a = carve(arena, a, T)
        w_, a = carve(arena, a, T)
        l_, a = carve(arena, a, T)
        dt, a = carve(arena, a, 2, T)
        du, a = carve(arena, a, 2, T)
        dbu, a = carve(arena, a, NR, T)
        hs, a = carve(arena, a, 2, NR, T)
        hc, a = carve(arena, a, 2, NR, T)
        rep, a = carve(arena, a, 2, 2, NR, T)
        assert a <= ARENA
        EXTRA = 2 * T + 4 * TC * DM
        extra = sb("extra", [P, EXTRA])
        bc_sb, _ = carve(extra, 0, 2, T, rows=2 * NS)
        ga, a = carve(extra, 0, 2, T)
        h1, a = carve(extra, a, TC, DM)
        sq3, a = carve(extra, a, TC, DM)
        lg, a = carve(extra, a, TC, E)
        oh, a = carve(extra, a, TC, E)
        mx, a = carve(extra, a, TC)
        mx2, a = carve(extra, a, TC)
        assert a <= EXTRA
        xs0 = xs[:, 0].rearrange("p d w -> p (d w)")
        hid, a = carve(xs0, 0, NBLK, T)
        xfT, a = carve(xs0, a, T, rows=DM + 1)
        ohT, a = carve(xs0, a, T, rows=E)
        h1b, a = carve(xs0, a, TC, DM)
        xc3, a = carve(xs0, a, TC, DM)
        xf, a = carve(xs0, a, TC, DM)
        fin, a = carve(xs0, a, TC, DM)
        assert a <= 2 * PADW

        def conv_wT(d, k):
            return wT[:, 2 + 4 * d + k, :]

        def flat(ap):
            return ap.rearrange("p a b -> p (a b)")

        A = lambda n: ins["L0_attn_" + n]
        loads = []

        def load(dst, src):
            loads.append((dst, src))

        load(in_w, A("in_w").rearrange("(h c) j -> c h j", h=2))
        load(conv_w[:, 0, :], A("conv_w"))
        load(conv_b[:, 0:1], A("conv_b").rearrange("(c a) -> c a", a=1))
        for h in range(2):
            load(ln_g[DM * h:DM * h + DM], A("ln_g").rearrange("(c a) -> c a", a=1))
            load(ln_b[DM * h:DM * h + DM], A("ln_b").rearrange("(c a) -> c a", a=1))
        load(out_w, A("out_w"))
        for d, n in enumerate(DIRS):
            load(dir_w[:, d], A(n + "_in_w").rearrange("(h c) j -> c h j", h=2))
            load(conv_w[:, 1 + d, :], A(n + "_conv_w"))
            load(conv_b[:, 1 + d:2 + d], A(n + "_conv_b").rearrange("(c a) -> c a", a=1))
            load(xdt[:, d], A(n + "_xproj_w")[0:R, :])
            load(xbc[:, d], A(n + "_xproj_w")[R:R + 2 * NS, :])
            load(dt_w[:, d], A(n + "_dt_w"))
            load(dt_b[:, d:d + 1], A(n + "_dt_b").rearrange("(c a) -> c a", a=1))
            load(dskip[:, d:d + 1], A(n + "_D").rearrange("(c a) -> c a", a=1))
            load(dir_ow[:, d], A(n + "_out_w"))
            for m in range(4):
                load(alog[32 * m:32 * m + 32, d], A(n + "_Alog").rearrange("(q d) s -> d q s", d=32))
        F = lambda n: ins["L0_ffn_" + n]
        load(router_w, F("router_w"))
        load(router_wT[DM:DM + 1, :], F("router_b").rearrange("(a e) -> a e", a=1))
        load(w1[:], F("W1").rearrange("e d h -> d e h"))
        load(b1[:], F("b1").rearrange("e h -> (e h)").rearrange("(n p) -> p n", p=P))
        load(w2[:], F("W2").rearrange("e h d -> (e h) d").rearrange("(n p) d -> p n d", p=P))
        load(b2[:], F("b2"))

        block = ctx.enter_context(nc.Block())
        NLN = 2 * B

        PAIR = 2 * NQ * NR

        def bank(d, tile):
            return 3 + (NQ * NR * d + tile) % 3

        def bank_age(d, tile):
            at = NQ * NR * d + tile
            return next(n for n in range(1, PAIR) if (at - n) % PAIR % 3 == at % 3)

        SIDE, SIDE2 = 2, 7

        def xs_at(b, i, d, shift=0):
            return xs[:, b, d, bass.ds((i - CB * b) * T + shift, T)]

        def wait(eng, name, value):
            if not (isinstance(value, int) and value <= 0):
                eng.wait_ge(sem(name), value)

        def phases(eng, pair, loop=None):
            for b in range(B):
                pair(b, CB * b)
                if loop:
                    loop(CB * b + 1, CB * b + CB - 1, b)
                else:
                    with eng.Fori(CB * b + 1, CB * b + CB - 1) as i:
                        pair(b, i)
                pair(b, CB * b + CB - 1)

        @block.sync
        def _(sp):
            sp.dma_start(ids[:], x.rearrange("b (t p) -> (b t) p", p=P)).then_inc(sem("ids_in"), 16)
            with nc.allow_non_contiguous_dma(reason="b1 is 2 KB"):
                for dst, src in loads:
                    sp.dma_start(dst, src).then_inc(sem("weights_in"), 16)

            def store_bc(n, d):
                sp.wait_ge(sem("bc_in_sbuf"), 2 * n + d + 1)
                sp.dma_start(bc_dram[d, :, bass.ds(n * T, T)], bc_sb[:, d, :]) \
                  .then_inc(sem(f"bc_in_dram_{DIRS[d]}"), 16)

            def load_rep(i, d):
                sp.wait_ge(sem(f"bc_in_dram_{DIRS[d]}"), 16 * (i + 1))
                wait(sp, "hc_ready", NQ * (2 * i + d) - NQ if not (isinstance(i, int) and i == 0) else 0)
                for m in range(4):
                    src = bc_dram[d].rearrange("(k m) t -> m k t", m=4)[m]
                    src = src.unsqueeze(0).broadcast_to([32, 2 * NR, NTOK])[:, :, bass.ds(i * T, T)]
                    sp.dma_start(rep[32 * m:32 * m + 32, d].rearrange("p a b t -> p (a b) t"), src) \
                      .then_inc(sem(f"rep_in_{DIRS[d]}"), 16)

            def store(n):
                sp.wait_ge(sem("fin_ready"), n + 2)
                sp.dma_start(out.rearrange("b (t p) d -> p (b t) d", p=P)[:, bass.ds(n * TC, TC), :], fin) \
                  .then_inc(sem("out_done"), 16)

            with sp.Fori(0, CB) as n:
                for d in range(2):
                    store_bc(n, d)
            for d in range(2):
                load_rep(0, d)

            def pair_0(i):
                for d in range(2):
                    store_bc(CB + i, d)
                    load_rep(i + 1, d)
            with sp.Fori(0, CB) as i:
                pair_0(i)
            def pair_1(i, stored):
                load_rep(i + 1, 0)
                if stored:
                    store(i - CB - 1)
                load_rep(i + 1, 1)
            pair_1(CB, False)
            with sp.Fori(CB + 1, NCH - 1) as i:
                pair_1(i, True)
            with sp.Fori(CB - 2, NCH) as n:
                store(n)
            sp.wait_ge(sem("out_done"), 16 * (NCH + 1))

        @block.gpsimd
        def _(pool):
            ch = Chain(pool, sem("pool_step"))

            def fill_where(view, pattern, base, fill):
                ch.step(pool.affine_select(out=view, in_=view, compare_op=ALU.not_equal, fill=fill,
                                           base=base, pattern=pattern, channel_multiplier=1))

            ch.step(pool.memset(ident[:], 0.0))
            fill_where(ident[:], [[-1, P]], 0, 1.0)
            pool.memset(fold[:], 0.0).then_inc(sem("ident_ready"), 1)
            pool.wait_ge(sem("ident_ready"), 1)
            for m in range(4):
                fill_where(fold[:], [[-1, 32]], -32 * m, 1.0)
            ch.step(pool.memset(pickf, 0.0))
            fill_where(pickf.rearrange("p n (e h) -> p n e h", h=H),
                       [[-(P // H), NBLK], [-1, P // H], [0, H]], 0, BIG)
            ch.step(pool.memset(pickf[E:E + 1], -BIG))
            ch.step(pool.iota(ranki[:], pattern=[[-1, E]], base=E, channel_multiplier=0))
            ch.step(pool.memset(eps[:], EPS))
            pool.memset(lns[:], 0.0).then_inc(sem("consts"), 1)

            rows = table.rearrange("v (s d) -> (v s) d", d=DM)
            pool.wait_ge(sem("idx_ready"), 1)
            for t in range(TILES):
                pool.indirect_dma_start(
                    out=x0[:, t, :], out_offset=None, in_=rows,
                    in_offset=bass.IndirectOffsetOnAxis(ap=idx[:, t:t + 1], axis=0),
                ).then_inc(sem(f"gathered_{t // TB}"), 16)

            def softplus(unit, d):
                pool.wait_ge(sem("sp_c"), unit + 1)
                pool.tensor_tensor(l_, l_, e_, ALU.subtract).then_inc(sem("sp_log1p"), 1)
                pool.wait_ge(sem("sp_log1p"), unit + 1)
                pool.tensor_tensor(dt[:, d], v_, l_, ALU.add).then_inc(sem("dt_ready"), 1)

            def by_c(i, d, q, first=False):
                done = NQ * (2 * i + d) + q
                if q == 0:
                    pool.wait_ge(sem(f"rep_in_{DIRS[d]}"), 64 * (i + 1))
                if not (first and d == 0 and q < 2):
                    pool.wait_ge(sem("summed"), done - 1)
                pool.wait_ge(sem("scans"), NR * (done + 1))
                pool.tensor_tensor(flat(hc[:, q % 2]), flat(hs[:, q % 2]), flat(rep[:, d, 1]), ALU.mult) \
                    .then_inc(sem("hc_ready"), 1)

            def pair(b, i):
                const = isinstance(i, int)
                for d in range(2):
                    for q in range(NQ):
                        by_c(i, d, q, first=(const and i == 0))
                        if q == 0 and not (const and i == NCH - 1 and d == 1):
                            softplus(2 * i + d + 1, 1 - d)

            softplus(0, 0)
            phases(pool, pair)

        @block.tensor
        def _(pe):
            pe.wait_ge(sem("ident_ready"), 1)
            pe.wait_ge(sem("ids_clamped"), 1)
            pe.transpose(ps[:, 6, 0:TILES], idx_f, ident[0:TILES, 0:TILES]).then_inc(sem("idx_ps"), 1)

            pe.wait_ge(sem("weights_in"), 16 * len(loads))
            pe.wait_ge(sem("taps_ready"), 1)

            def turn(slot, src, at=0):
                k, m = src.shape[0], src.shape[1]
                return pe.transpose(ps[0:m, slot // 4, (slot % 4) * P + at:(slot % 4) * P + at + k],
                                    src, ident[0:k, 0:k])

            for s in range(2):
                turn(s, flat(taps[:, s]))
            for d in range(2):
                for k in range(4):
                    turn(2 + 4 * d + k, dir_taps[:, d, k])
            for d in range(2):
                turn(10 + d, dir_w[:, d, 1])
                turn(12 + d, dir_ow[:, d])
                turn(14, out_w[:, P * d:P * d + P], at=DM * d)
                turn(15, xbc[:, d], at=2 * NS * d)
            turn(16, in_w[:, 1])
            turn(17, router_w)
            for d in range(2):
                mm = turn(18 + d, dt_w[:, d])
            mm.then_inc(sem("wT_ps"), 1)
            pe.wait_ge(sem("wT_ready"), 1)
            for d in range(2):
                mm = pe.matmul(ps[:, 5, P * d:P * d + P], xdt[:, d], dt_wT[:, d], start=True, stop=True)
            mm.then_inc(sem("dtproj_ps"), 1)
            pe.wait_ge(sem("wT_ready"), 2)

            def stage_a1(b):
                pe.wait_ge(sem("u2_ready"), b + 1)
                def turn_chunk(c):
                    n = CB * b + c
                    if n >= 2:
                        pe.wait_ge(sem("uT_act"), n - 1)
                        pe.wait_ge(sem("uT_dve"), n - 1)
                    for t in range(TC):
                        tr = pe.transpose(ps[:, c % 2, t * P:t * P + P], flat(u2d[:, TC * c + t]), ident[:])
                    tr.then_inc(sem("turned"), 1)
                turn_chunk(0)
                for c in range(CB):
                    n = CB * b + c
                    if c + 1 < CB:
                        turn_chunk(c + 1)
                    pe.wait_ge(sem("uT_act"), n + 1)
                    pe.wait_ge(sem("uT_dve"), n + 1)
                    if n >= 2:
                        pe.wait_ge(sem("act_r_ready"), n - 1)
                        pe.wait_ge(sem("gate_ready"), n - 1)
                    for s in range(2):
                        mm = pe.matmul(ps[:, 2 + c % 2, :], wT[:, s, :],
                                       uT[:, b, c * T + 3 - 2 * s:c * T + 3 - 2 * s + T],
                                       start=(s == 0), stop=(s == 1))
                    mm.then_inc(sem("x_ps"), 1)
                    pe.matmul(ps[:, 4 + c % 2, :], gate_wT[:], uT[0:DM, b, c * T + 3:c * T + 3 + T],
                              start=True, stop=True).then_inc(sem("gate_ps"), 1)

            def a2_conv(b, n, d):
                wait(pe, "bc_in_sbuf", 2 * n + d)
                for k in range(4):
                    mm = pe.matmul(ps[:, SIDE, :], conv_wT(d, k), xs_at(b, n, d, k),
                                   start=(k == 0), stop=(k == 3))
                mm.then_inc(sem("xs_ps"), 1)

            def a2_z(b, n, d, free):
                wait(pe, *free)
                pe.matmul(ps[:, SIDE2, :], wT[:, 10 + d, :], xs_at(b, n, d, 3),
                          start=True, stop=True).then_inc(sem("z_ps"), 1)

            def a2_bc(b, n, d):
                pe.wait_ge(sem("xs_ready"), 2 * n + d + 1)
                pe.matmul(ps[:, SIDE, :], wT[:, 15, :],
                          xs_at(b, n, d), start=True, stop=True).then_inc(sem("bc_ps"), 1)

            def stage_a2(n):
                for d in range(2):
                    a2_conv(0, n, d)
                    a2_z(0, n, d, ("z_ready", 2 * n + d))
                    a2_bc(0, n, d)

            stage_a1(0)
            pe.wait_ge(sem("act_ready"), CB)
            pe.wait_ge(sem("act_r_ready"), CB)
            pe.wait_ge(sem("gate_ready"), CB)
            stage_a2(0)
            with pe.Fori(1, CB) as n:
                stage_a2(n)
            pe.wait_ge(sem("bc_in_sbuf"), 2 * CB)
            stage_a1(1)

            def pre(b, i, d, free):
                wait(pe, *free)
                pe.matmul(ps[:, SIDE2, :], dtproj[:, d, :], xs_at(b, i, d), start=True, stop=True) \
                  .then_inc(sem("pre_ps"), 1)

            def spread_group(i, d, q):
                done = NQ * (2 * i + d) + q
                if q == 0:
                    pe.wait_ge(sem("du_ready"), 2 * i + d + 1)
                wait(pe, "dbu_ready", done)
                pe.matmul(ps[:, 1, :], spread[:, q, :], du[:, d], start=True, stop=True) \
                  .then_inc(sem("du_spread"), 1)
                if q == 0:
                    pe.wait_ge(sem("dt_ready"), 2 * i + d + 1)
                wait(pe, "decay_ready", NR * done)
                pe.matmul(ps[:, 0, :], spread[:, q, :], dt[:, d], start=True, stop=True) \
                  .then_inc(sem("dt_spread"), 1)

            def nsum(b, i, d, q):
                if q == 0:
                    wait(pe, "yz_ready", 2 * i + d)
                    pe.matmul(ps[:, 6, :], skip[:, d, :], xs_at(b, i, d),
                              start=True, stop=False, skip_group_check=True)
                pe.wait_ge(sem("hc_ready"), NQ * (2 * i + d) + q + 1)
                for r in range(NR):
                    mm = pe.matmul(ps[32 * q:32 * q + 32, 6, :], fold[:], hc[:, q % 2, r],
                                   start=False, stop=(r == NR - 1), skip_group_check=True)
                mm.then_inc(sem("summed"), 1)

            def c_front(n, s, back, units, free):
                if s == 1:
                    wait(pe, *free)
                    pe.wait_ge(sem("yz_ready"), units - 1)
                    pe.matmul(ps[:, SIDE2, :], wT[:, 12, :], z[:, 0, bass.ds(n * T, T)],
                              start=True, stop=True).then_inc(sem("dir_out"), 1)
                if s == 2:
                    pe.wait_ge(sem("gated"), 2 * n + 1)
                    pe.wait_ge(sem("yz_ready"), units)
                    pe.matmul(ps[:, SIDE2, :], wT[:, 13, :], z[:, 1, bass.ds(back, T)],
                              start=True, stop=True).then_inc(sem("dir_out"), 1)
                if s == 3:
                    pe.wait_ge(sem("gated"), 2 * n + 2)
                    for t in range(TC):
                        for d in range(2):
                            mm = pe.matmul(ps[:, SIDE2, t * DM:t * DM + DM], ga[:, d, t * P:t * P + P],
                                           wT[:, 14, DM * d:DM * d + DM], start=(d == 0), stop=(d == 1))
                    mm.then_inc(sem("attn_ps"), 1)

            def c_front_end(n, s, free=None):
                if s == 6:
                    if free:
                        wait(pe, *free)
                    pe.wait_ge(sem("xf_ready"), n + 1)
                    for h in range(TC // 2):
                        tr = pe.transpose(ps[:, SIDE2, h * P:h * P + P], flat(xf[:, 2 * h:2 * h + 2]), ident[:])
                    tr.then_inc(sem("xfT_ps"), 1)
                if s == 7:
                    pe.wait_ge(sem("xfT_ready"), 2 * n + 2)
                    for t in range(TC):
                        mm = pe.matmul(ps[:, SIDE2, t * E:t * E + E], xfT[:, t * P:t * P + P], router_wT[:],
                                       start=True, stop=True)
                    mm.then_inc(sem("logits_ps"), 1)

            def c_back(n, s):
                if s == 0:
                    pe.wait_ge(sem("choice_ready"), n + 1)
                    pe.wait_ge(sem("fin_ready"), n + 1)
                    for t in range(TC):
                        tr = pe.transpose(ps[0:E, SIDE, t * P:t * P + P], oh[:, t], ident[:])
                    tr.then_inc(sem("choice_ps"), 1)
                if 1 <= s <= NBLK:
                    k = s - 1
                    if k == 0:
                        pe.wait_ge(sem("choiceT_bf16"), n + 1)
                    else:
                        pe.wait_ge(sem("hidden"), NBLK * n + k)
                    pe.matmul(ps[:, SIDE, :], pick[:, k, :], ohTb[:], start=True, stop=False)
                    pe.matmul(ps[:, SIDE, :], w1[:, 8 * k:8 * k + 8, :].rearrange("p e h -> p (e h)"),
                              xfT[0:DM, :], start=False, stop=True).then_inc(sem("hidden_ps"), 1)
                if s in (5, 6):
                    pe.wait_ge(sem("hidden"), NBLK * n + NBLK)
                    for t in range(2 * (s - 5), 2 * (s - 5) + 2):
                        for k in range(NBLK):
                            pe.matmul(ps[:, SIDE, t * DM:t * DM + DM], hid[:, k, t * P:t * P + P], w2[:, k, :],
                                      start=(k == 0), stop=False)
                        mm = pe.matmul(ps[:, SIDE, t * DM:t * DM + DM], ohT[:, t * P:t * P + P], b2[:],
                                       start=False, stop=True)
                    if s == 6:
                        mm.then_inc(sem("moe_ps"), 1)

            def pair(b, i):
                const = isinstance(i, int)
                for s in range(2 * NQ):
                    d, q = divmod(s, NQ)
                    spread_group(i, d, q)
                    if q >= 2:
                        nsum(b, i, d, q - 2)
                    elif d:
                        nsum(b, i, 0, q + 2)
                    elif not (const and i == 0):
                        nsum(b - 1 if const and i == CB * b else b, i - 1, 1, q + 2)
                    if q == 0 and not (const and i == NCH - 1 and d):
                        b_next = b + 1 if const and i == CB - 1 and d else b
                        n = CB + i
                        free = ("z_ready", 2 * n + d) if b == 0 else \
                               ("h1_sum", i - CB + 1) if d else \
                               ("z_ready", UNITS) if const and i == CB else ("logits_read", i - CB)
                        pre(b_next, i + d, 1 - d, free)
                    read = ("softplus_a", 2 * i + d + 2)
                    if b == 0:
                        n = CB + i
                        if q == 0:
                            a2_conv(1, n, d)
                        if q == 2:
                            a2_z(1, n, d, read)
                        if q == 3:
                            a2_bc(1, n, d)
                    else:
                        n = i - CB
                        if not (const and i == CB):
                            c_back(n - 1, s)
                        c_front(n, s, n * -T + (CB - 1) * T, 2 * CB, read)
                        c_front_end(n, s, None if const and i == NCH - 1 else read)

            pe.wait_ge(sem("z_ready"), 2 * CB)
            pe.wait_ge(sem("act_ready"), NCH)
            pe.wait_ge(sem("act_r_ready"), NCH)
            pe.wait_ge(sem("gate_ready"), NCH)
            pre(0, 0, 0, ("z_ready", 2 * CB))
            phases(pe, pair)
            nsum(1, NCH - 1, 1, 2)
            nsum(1, NCH - 1, 1, 3)

            with pe.Fori(CB, NCH) as n:
                for s in range(8):
                    c_back(n - 1, s)
                    c_front(n, s, n * -T + (CB - 1) * T + 2 * L, UNITS, ("logits_read", n))
                    c_front_end(n, s)
            for s in range(7):
                c_back(NCH - 1, s)

        @block.scalar
        def _(act_e):
            def ln_squares(ordinal, xc, sq):
                act_e.wait_ge(sem("ln_centred"), ordinal)
                act_e.activation(sq, xc, ACT.Square).then_inc(sem("ln_squares"), 1)

            def ln_rsqrt(ordinal, width):
                act_e.wait_ge(sem("ln_sumsq"), ordinal)
                act_e.activation(lns[:, 2, 0:width], lns[:, 1, 0:width], ACT.Ln, scale=1.0 / DM,
                                 bias=eps[:, 0:1]).then_inc(sem("ln_log"), 1)
                act_e.wait_ge(sem("ln_log"), ordinal)
                act_e.activation(lns[:, 3, 0:width], lns[:, 2, 0:width], ACT.Exp, scale=-0.5) \
                     .then_inc(sem("ln_rsqrt"), 1)

            def exp_ln_tables():
                act_e.preload_act_table_set("natural_log_exp_and_others")

            exp_ln_tables()
            act_e.wait_ge(sem("weights_in"), 16 * len(loads))
            for m in range(4):
                rows = slice(32 * m, 32 * m + 32)
                act_e.activation(negA[rows].rearrange("p a b c -> p (a b) c"),
                                 alog[rows].rearrange("p a b (r m) -> p (a b) r m", m=4)[:, :, :, m],
                                 ACT.Exp).then_inc(sem("expA"), 1)
            act_e.wait_ge(sem("consts"), 1)

            def stage_a1(b):
                with act_e.Fori(0, CB // 2) as c2:
                    for k in range(2):
                        n = CB * b + 2 * c2 + k
                        at = (2 * c2 + k) * T
                        act_e.wait_ge(sem("turned"), n + 1)
                        act_e.activation(uT[0:DM, b, bass.ds(at + 3, T)], ps[0:DM, k, :], ACT.Identity,
                                         scale=ln_g[0:DM, 0:1], bias=ln_b[0:DM, 0:1]) \
                             .then_inc(sem("uT_act"), 1)
                        act_e.wait_ge(sem("x_ps"), n + 1)
                        act_e.activation(xs[:, b, 0, bass.ds(at + 3, T)], ps[:, 2 + k, :], ACT.Silu,
                                         bias=conv_b[:, 0:1]).then_inc(sem("act_ready"), 1)
                        act_e.activation(xs[:, b, 1, bass.ds(L - T + 3 - at, T)], ps[:, 2 + k, REV], ACT.Silu,
                                         bias=conv_b[:, 0:1]).then_inc(sem("act_r_ready"), 1)
                        act_e.wait_ge(sem("gate_ps"), n + 1)
                        act_e.activation(gate[:, bass.ds(n * T, T)], ps[:, 4 + k, :], ACT.Silu) \
                             .then_inc(sem("gate_ready"), 1)

            def a2_silus(b, n, d):
                act_e.wait_ge(sem("xs_ps"), 2 * n + d + 1)
                act_e.wait_ge(sem("z_ps"), 2 * n + d + 1)
                act_e.activation(xs_at(b, n, d), ps[:, SIDE, :], ACT.Silu,
                                 bias=conv_b[:, 1 + d:2 + d]).then_inc(sem("xs_ready"), 1)
                act_e.activation(z[:, d, bass.ds(n * T, T)], ps[:, SIDE2, :], ACT.Silu) \
                     .then_inc(sem("z_ready"), 1)

            def stage_a2(n):
                for d in range(2):
                    a2_silus(0, n, d)
                    act_e.wait_ge(sem("bc_ps"), 2 * n + d + 1)
                    wait(act_e, f"bc_in_dram_{DIRS[d]}", 16 * n)
                    act_e.activation(bc_sb[:, d, :], ps[2 * NS * d:2 * NS * d + 2 * NS, SIDE, :], ACT.Copy) \
                         .then_inc(sem("bc_in_sbuf"), 1)

            def layernorm(ordinal):
                ln_squares(ordinal, flat(xc), flat(sq))
                ln_rsqrt(ordinal, TB)

            layernorm(1)
            layernorm(2)
            stage_a1(0)
            for n in range(2):
                stage_a2(n)
                exp_ln_tables()
                layernorm(3 + n)
            with act_e.Fori(2, CB) as n:
                stage_a2(n)
            stage_a1(1)
            exp_ln_tables()

            def softplus(i, d, first=False):
                unit = 2 * i + d
                if not first:
                    act_e.wait_ge(sem("dt_ready"), unit)
                act_e.wait_ge(sem("pre_ps"), unit + 1)
                act_e.activation(v_, ps[:, SIDE2, :], ACT.Relu, bias=dt_b[:, d:d + 1])
                act_e.activation(w_, ps[:, SIDE2, :], ACT.Abs, bias=dt_b[:, d:d + 1]).then_inc(sem("softplus_a"), 1)
                act_e.wait_ge(sem("softplus_a"), unit + 1)
                act_e.activation(e_, w_, ACT.Exp, scale=-1.0).then_inc(sem("softplus_e"), 1)
                act_e.wait_ge(sem("softplus_e"), unit + 1)
                act_e.activation(w_, e_, ACT.Identity, bias=1.0).then_inc(sem("softplus_w"), 1)
                act_e.wait_ge(sem("softplus_w"), unit + 1)
                act_e.activation(l_, w_, ACT.Ln).then_inc(sem("softplus_l"), 1)

            def decays(i, d, q, first):
                done = NQ * (2 * i + d) + q
                act_e.wait_ge(sem("dt_spread"), done + 1)
                for r in range(NR):
                    tile = NR * q + r
                    if not (first and d == 0 and tile < 3):
                        act_e.wait_ge(sem("scans"), NR * done + r + 1 - bank_age(d, tile))
                    act_e.activation(ps[:, bank(d, tile), :], ps[:, 0, :], ACT.Exp,
                                     scale=negA[:, d, q, r:r + 1]).then_inc(sem("decay_ready"), 1)

            def c_front(n, s):
                if s == 3:
                    ln_squares(NLN + n + 1, flat(xc3), flat(sq3))
                if s == 4:
                    ln_rsqrt(NLN + n + 1, TC)
                if s == 6:
                    act_e.wait_ge(sem("xfT_ps"), n + 1)
                    for h in range(2):
                        act_e.activation(
                            xfT[0:DM, :].rearrange("p (g h t) -> p g h t", h=2, t=P)[:, :, h],
                            ps[DM * h:DM * h + DM, SIDE2, 0:T // 2].rearrange("p (g t) -> p g t", t=P),
                            ACT.Copy).then_inc(sem("xfT_ready"), 1)

            def c_back(n, s):
                if s == 0:
                    act_e.wait_ge(sem("choiceT"), n + 1)
                    act_e.activation(ohTb[0:E, :], ohT, ACT.Copy).then_inc(sem("choiceT_bf16"), 1)
                if 1 <= s <= NBLK:
                    k = s - 1
                    act_e.wait_ge(sem("hidden_ps"), NBLK * n + k + 1)
                    act_e.activation(hid[:, k, :], ps[:, SIDE, :], ACT.Relu, bias=b1[:, k:k + 1]) \
                         .then_inc(sem("hidden"), 1)

            def pair(b, i):
                const = isinstance(i, int)
                for s in range(2 * NQ):
                    d, q = divmod(s, NQ)
                    decays(i, d, q, const and i == 0)
                    if q == 0 and not (const and i == NCH - 1 and d):
                        softplus(i + d, 1 - d)
                    if b == 0 and q == 2:
                        a2_silus(1, CB + i, d)
                        exp_ln_tables()
                    if b == 1:
                        if not (const and i == CB):
                            c_back(i - CB - 1, s)
                        c_front(i - CB, s)

            softplus(0, 0, first=True)
            phases(act_e, pair)
            with act_e.Fori(CB, NCH) as n:
                for s in range(8):
                    c_back(n - 1, s)
                    c_front(n, s)
            for s in range(5):
                c_back(NCH - 1, s)

        @block.vector
        def _(dve):
            ch = Chain(dve, sem("dve_step"))

            dve.wait_ge(sem("ids_in"), 16)
            ch.step(dve.tensor_copy(idx_f, ids[:]))
            ch.step(dve.tensor_scalar(idx_g, idx_f, 0.0, float(V), ALU.is_lt, ALU.mult))
            ch.step(dve.tensor_tensor(idx_g, idx_g, idx_f, ALU.add))
            ch.step(dve.tensor_scalar(idx_g, idx_g, 0.0, float(V - 1), ALU.max, ALU.min))
            dve.tensor_scalar(idx_f, idx_g, float(HID // DM), float(SLICE), ALU.mult, ALU.add) \
               .then_inc(sem("ids_clamped"), 1)
            dve.wait_ge(sem("idx_ps"), 1)
            dve.tensor_copy(idx[:], ps[:, 6, 0:TILES]).then_inc(sem("idx_ready"), 1)

            dve.wait_ge(sem("consts"), 1)
            dve.wait_ge(sem("weights_in"), 16 * len(loads))
            for k in range(4):
                ch.mark(dve.tensor_scalar(taps[:, (3 - k) // 2, (3 - k) % 2, :], in_w[:, 0, :],
                                          conv_w[:, 0, k:k + 1], None, ALU.mult))
                for d in range(2):
                    ch.mark(dve.tensor_scalar(dir_taps[:, d, k, :], dir_w[:, d, 0, :],
                                              conv_w[:, 1 + d, k:k + 1], None, ALU.mult))
            ch.wait()
            dve.tensor_copy(spread[:].rearrange("p q (n d) -> p q n d", d=32),
                            ident[:].rearrange("p (q d) -> p q d", d=32).unsqueeze(2)
                            .broadcast_to([P, NQ, 4, 32])).then_inc(sem("taps_ready"), 1)
            for d in range(2):
                ch.mark(dve.tensor_scalar(skip[:, d, :], ident[:], dskip[:, d:d + 1], None, ALU.mult))
            dve.wait_ge(sem("expA"), 4)
            ch.mark(dve.tensor_scalar(negA[:].rearrange("p a b c -> p (a b c)"),
                                      negA[:].rearrange("p a b c -> p (a b c)"), -1.0, None, ALU.mult))
            ch.mark(dve.tensor_copy(rank[:], ranki[:]))
            ch.mark(dve.tensor_copy(pick[:], pickf))
            dve.wait_ge(sem("wT_ps"), 1)
            for k in range(3):
                ch.mark(dve.tensor_copy(flat(wT[:, 4 * k:4 * k + 4, :]), ps[:, k, :]))
            ch.mark(dve.tensor_copy(flat(wT[:, 12:15, :]), ps[:, 3, 0:3 * P]))
            ch.mark(dve.tensor_copy(wT[:, 15, 0:4 * NS], ps[:, 3, 3 * P:3 * P + 4 * NS]))
            ch.mark(dve.memset(wT[:, 15, 4 * NS:], 0.0))
            ch.mark(dve.tensor_copy(gate_wT[:], ps[0:DM, 4, 0:P]))
            ch.mark(dve.tensor_copy(router_wT[0:DM, :], ps[0:DM, 4, P:P + E]))
            ch.mark(dve.memset(uT[:, :, 0:4], 0.0))
            ch.mark(dve.memset(xs[:, :, :, 0:3], 0.0))
            ch.mark(dve.memset(carry[:].rearrange("p a b c -> p (a b c)"), 0.0))
            ch.wait()
            dve.tensor_copy(flat(dt_wT[:]), ps[0:R, 4, 2 * P:4 * P]).then_inc(sem("wT_ready"), 1)
            dve.wait_ge(sem("dtproj_ps"), 1)
            dve.tensor_copy(flat(dtproj[:]), ps[:, 5, 0:2 * P]).then_inc(sem("wT_ready"), 1)

            def small(k, width):
                return lns[:, k, 0:width]

            def ln_centre(src, xc, width):
                ch.step(dve.tensor_reduce(small(0, width), src, AX, ALU.add))
                ch.step(dve.tensor_scalar(small(0, width), small(0, width), 1.0 / DM, None, ALU.mult))
                dve.tensor_tensor(xc, src, small(0, width).unsqueeze(2).broadcast_to([P, width, DM]),
                                  ALU.subtract).then_inc(sem("ln_centred"), 1)

            def ln_var(ordinal, sq, width):
                dve.wait_ge(sem("ln_squares"), ordinal)
                dve.tensor_reduce(small(1, width), sq, AX, ALU.add).then_inc(sem("ln_sumsq"), 1)
                dve.wait_ge(sem("ln_sumsq"), ordinal)
                ch.mark(dve.tensor_scalar(small(4, width), small(1, width), 1.0 / DM, EPS, ALU.mult, ALU.add))

            def ln_scale(ordinal, xc, width, outs):
                dve.wait_ge(sem("ln_rsqrt"), ordinal)
                r, t, y = small(3, width), small(5, width), small(6, width)
                ch.step(dve.tensor_tensor(t, r, r, ALU.mult))
                ch.step(dve.tensor_tensor(t, t, small(4, width), ALU.mult))
                ch.step(dve.tensor_scalar(t, t, -0.5, 1.5, ALU.mult, ALU.add))
                ch.step(dve.tensor_tensor(y, t, r, ALU.mult))
                wide = y.unsqueeze(2).broadcast_to([P, width, DM])
                for o in outs[:-1]:
                    ch.mark(dve.tensor_tensor(o, xc, wide, ALU.mult))
                return dve.tensor_tensor(outs[-1], xc, wide, ALU.mult)
            LN_STEPS = 7

            for b in range(B):
                dve.wait_ge(sem(f"gathered_{b}"), 16 * TB)
                xb = x0[:, TB * b:TB * b + TB, :]
                ln_centre(xb, xc, TB)
                ln_var(2 * b + 1, sq, TB)
                ch.step(ln_scale(2 * b + 1, xc, TB, [u]))
                ln_centre(u, xc, TB)
                ch.mark(dve.tensor_tensor(xb, xb, u, ALU.add))
                ln_var(2 * b + 2, sq, TB)
                if b:
                    dve.wait_ge(sem("turned"), CB * b)
                ln_scale(2 * b + 2, xc, TB, [u2d[:, :, 0, :], u2d[:, :, 1, :]]).then_inc(sem("u2_ready"), 1)
                with dve.Fori(0, CB // 2) as c2:
                    for k in range(2):
                        n = CB * b + 2 * c2 + k
                        dve.wait_ge(sem("turned"), n + 1)
                        dve.tensor_scalar(uT[DM:P, b, bass.ds((2 * c2 + k) * T + 4, T)], ps[DM:P, k, :],
                                          ln_g[DM:P, 0:1], ln_b[DM:P, 0:1], ALU.mult, ALU.add) \
                           .then_inc(sem("uT_dve"), 1)

            def softplus_c(unit):
                dve.wait_ge(sem("softplus_l"), unit + 1)
                dve.scalar_tensor_tensor(e_, w_, -1.0, e_, ALU.add, ALU.subtract).then_inc(sem("sp_c"), 1)

            def dt_times_u(b, i, d):
                dve.wait_ge(sem("dt_ready"), 2 * i + d + 1)
                dve.tensor_tensor(du[:, d], dt[:, d], xs_at(b, i, d), ALU.mult).then_inc(sem("du_ready"), 1)

            def keep_last(g, d, q, reset):
                dve.wait_ge(sem("scans"), NR * g + NR)
                if reset:
                    ins = dve.memset(carry[:, d, q], 0.0)
                else:
                    ins = dve.tensor_copy(carry[:, d, q], hs[:, q % 2, :, T - 1])
                ins.then_inc(sem("carried"), 1)

            def group(b, i, d, q):
                const = isinstance(i, int)
                g = NQ * (2 * i + d) + q
                at = NQ * d + q
                if at:
                    keep_last(g - 1, (at - 1) // NQ, (at - 1) % NQ, const and i == CB - 1)
                elif not (const and i == 0):
                    keep_last(g - 1, 1, NQ - 1, const and i == CB)
                dve.wait_ge(sem("du_spread"), g + 1)
                if q == 0:
                    dve.wait_ge(sem(f"rep_in_{DIRS[d]}"), 64 * (i + 1))
                dve.tensor_tensor(dbu, ps[:, 1, :].unsqueeze(1).broadcast_to([P, NR, T]), rep[:, d, 0],
                                  ALU.mult).then_inc(sem("dbu_ready"), 1)
                if not (const and i == 0):
                    dve.wait_ge(sem("carried"), g - 2 * NQ + 1)
                if not (const and g < 2):
                    dve.wait_ge(sem("hc_ready"), g - 1)
                dve.wait_ge(sem("dbu_ready"), g + 1)
                for r in range(NR):
                    dve.wait_ge(sem("decay_ready"), NR * g + r + 1)
                    dve.tensor_tensor_scan(hs[:, q % 2, r], ps[:, bank(d, NR * q + r), :], dbu[:, r],
                                           carry[:, d, q, r:r + 1], ALU.mult, ALU.add) \
                       .then_inc(sem("scans"), 1)

            def y_by_z(i, d):
                unit = 2 * i + d
                dve.wait_ge(sem("summed"), NQ * unit + NQ)
                zc = z[:, d, bass.ds(i * T, T)]
                dve.tensor_tensor(zc, ps[:, 6, :], zc, ALU.mult).then_inc(sem("yz_ready"), 1)

            def bc_out(n, d):
                dve.wait_ge(sem("bc_ps"), 2 * n + d + 1)
                dve.wait_ge(sem(f"bc_in_dram_{DIRS[d]}"), 16 * n)
                dve.tensor_copy(bc_sb[:, d, :], ps[2 * NS * d:2 * NS * d + 2 * NS, SIDE, :]).then_inc(sem("bc_in_sbuf"), 1)

            def c_front(n, s):
                if s in (1, 2):
                    d = s - 1
                    dve.wait_ge(sem("dir_out"), 2 * n + d + 1)
                    if d == 0:
                        wait(dve, "attn_ps", n)
                    dve.tensor_tensor(ga[:, d], ps[:, SIDE2, :] if d == 0 else ps[:, SIDE2, REV],
                                      gate[:, bass.ds(n * T, T)], ALU.mult).then_inc(sem("gated"), 1)
                if s == 3:
                    dve.wait_ge(sem("attn_ps"), n + 1)
                    dve.tensor_tensor(flat(h1), ps[:, SIDE2, 0:TC * DM], flat(x0[:, bass.ds(n * TC, TC), :]),
                                      ALU.add).then_inc(sem("h1_sum"), 1)
                    dve.wait_ge(sem("h1_sum"), n + 1)
                    ln_centre(h1, xc3, TC)
                if s == 4:
                    ln_var(NLN + n + 1, sq3, TC)
                if s == 5:
                    ln_scale(NLN + n + 1, xc3, TC, [xf]).then_inc(sem("xf_ready"), 1)
                if s == 7:
                    dve.wait_ge(sem("logits_ps"), n + 1)
                    dve.tensor_copy(flat(lg), ps[:, SIDE2, 0:TC * E]).then_inc(sem("logits_read"), 1)
                    dve.wait_ge(sem("logits_read"), n + 1)
                    ch.step(dve.tensor_reduce(mx, lg, AX, ALU.max))
                    ch.step(dve.tensor_tensor(lg, lg, mx.unsqueeze(2).broadcast_to([P, TC, E]), ALU.is_equal))
                    ch.step(dve.tensor_tensor(lg, lg, rank[:].unsqueeze(1).broadcast_to([P, TC, E]), ALU.mult))
                    ch.step(dve.tensor_reduce(mx2, lg, AX, ALU.max))
                    dve.tensor_tensor(oh, lg, mx2.unsqueeze(2).broadcast_to([P, TC, E]), ALU.is_equal) \
                       .then_inc(sem("choice_ready"), 1)
                    ch.mark(dve.tensor_copy(h1b, h1))
            FRONT_MARKS = LN_STEPS + 5

            def c_back(n, s):
                if s == 0:
                    dve.wait_ge(sem("choice_ps"), n + 1)
                    dve.tensor_copy(ohT, ps[0:E, SIDE, :]).then_inc(sem("choiceT"), 1)
                if s == 6:
                    dve.wait_ge(sem("moe_ps"), n + 1)
                    dve.wait_ge(sem("out_done"), 16 * (n + 1))
                    dve.scalar_tensor_tensor(flat(fin), ps[:, SIDE, 0:TC * DM], 0.0, flat(h1b),
                                             ALU.max, ALU.add).then_inc(sem("fin_ready"), 1)

            def pair(b, i):
                const = isinstance(i, int)
                last = const and i == NCH - 1
                for s in range(2 * NQ):
                    d, q = divmod(s, NQ)
                    group(b, i, d, q)
                    if q == 1:
                        if d:
                            y_by_z(i, 0)
                        elif not (const and i == 0):
                            y_by_z(i - 1, 1)
                        if not (last and d):
                            softplus_c(2 * i + d + 1)
                    if q == 2 and not (last and d):
                        dt_times_u(b + 1 if const and i == CB - 1 and d else b, i + d, 1 - d)
                    if b == 0 and q == 3:
                        bc_out(CB + i, d)
                    if b == 1:
                        if not (const and i == CB):
                            c_back(i - CB - 1, s)
                        elif s in (1, 2):
                            dve.wait_ge(sem(f"bc_in_dram_{DIRS[s - 1]}"), 16 * NCH)
                        c_front(i - CB, s)
                if const and i == CB - 1:
                    dve.wait_ge(sem("summed"), NQ * (2 * i + 2) - 2)
                    ch.step(dve.memset(xfT[DM:DM + 1, :], 1.0))
                    dve.memset(fin, 0.0).then_inc(sem("out_done"), 16)
                    dve.wait_ge(sem("out_done"), 16)
                    dve.memset(ohTb[E:E + 1, :], 1.0).then_inc(sem("fin_ready"), 1)

            def loop(start, end, b):
                ch.loop(start, end, lambda i: pair(b, i), FRONT_MARKS if b else 0)

            softplus_c(0)
            dt_times_u(0, 0, 0)
            phases(dve, pair, loop)
            y_by_z(NCH - 1, 1)

            def chunk(n):
                for s in range(8):
                    c_back(n - 1, s)
                    c_front(n, s)

            ch.loop(CB, NCH, chunk, FRONT_MARKS)
            for s in range(7):
                c_back(NCH - 1, s)


_INS = ["x", "L0_tok_ple_table"] + ["L0_attn_" + n for n in (
    "ln_g", "ln_b", "in_w", "conv_w", "conv_b", "out_w")] + [
    f"L0_attn_{d}_{n}" for d in "fb" for n in (
        "in_w", "conv_w", "conv_b", "xproj_w", "dt_w", "dt_b", "Alog", "D", "out_w")] + [
    "L0_ffn_" + n for n in ("router_w", "router_b", "W1", "b1", "W2", "b2")]


def kernel(**inputs):
    import concourse.bacc as _bacc
    from concourse.bass_utils import run_bass_kernel_spmd as _run

    nc = _bacc.Bacc("TRN2", target_bir_lowering=False, num_devices=1)
    arrays, aps = {}, {}
    for name in _INS:
        a = np.ascontiguousarray(inputs[name])
        arrays[f"in_{name}"] = a
        aps[name] = nc.dram_tensor(f"in_{name}", a.shape, mybir.dt.from_np(a.dtype), kind="ExternalInput").ap()
    B, L = inputs["x"].shape
    out = nc.dram_tensor("out_h", (B, L, inputs["L0_attn_ln_g"].shape[0]), F32, kind="ExternalOutput").ap()
    build(nc, aps, out)
    r = _run(nc, [arrays], core_ids=[0])
    return r.results[0]["out_h"]
```

```python
from contextlib import ExitStack

import numpy as np

import concourse.bass as bass
from concourse import mybir
from concourse.alu_op_type import AluOpType as ALU

ACT = mybir.ActivationFunctionType
F32 = mybir.dt.float32
BF16 = mybir.dt.bfloat16
I32 = mybir.dt.int32
AX = mybir.AxisListType.X

P = 128
T = 512
NQ = 4
NR = 4
BIG = float(2.0 ** 120)
EPS = 1e-5
REV = slice(None, None, -1)


class Chain:

    def __init__(self, eng, sem):
        self.eng, self.sem, self.base, self.k = eng, sem, 0, 0

    def mark(self, ins):
        ins.then_inc(self.sem, 1)
        self.k += 1

    def wait(self):
        self.eng.wait_ge(self.sem, self.base + self.k)

    def step(self, ins):
        self.mark(ins)
        self.wait()

    def loop(self, start, end, body, per):
        base, k0 = self.base, self.k
        with self.eng.Fori(start, end) as i:
            self.base, self.k = base + k0 + (i - start) * per, 0
            body(i)
            assert self.k == per, self.k
        self.base, self.k = base, k0 + (end - start) * per


def build(nc, ins, out):
    x, table = ins["x"], ins["L0_tok_ple_table"]
    B, L = x.shape
    V, HID = table.shape
    DM = ins["L0_attn_ln_g"].shape[0]
    DH = ins["L0_attn_conv_w"].shape[0]
    NS = ins["L0_attn_f_Alog"].shape[1]
    R = ins["L0_attn_f_dt_w"].shape[1]
    E, _, H = ins["L0_ffn_W1"].shape
    SLICE = 3
    NTOK = B * L
    TILES = NTOK // P
    TB = TILES // B
    TC = T // P
    NCH = NTOK // T
    CB = L // T
    NBLK = E * H // P
    UNITS = 2 * NCH
    ARENA = 88 * 256
    DIRS = ("f", "b")
    assert DH == P and NQ * 32 == DH and NR * 4 == NS and 2 * DM == P

    with ExitStack() as ctx:
        def sb(name, shape, dt=F32):
            return ctx.enter_context(nc.sbuf_tensor(name, shape, dt))

        sems = {}

        def sem(name):
            if name not in sems:
                sems[name] = ctx.enter_context(nc.semaphore(name))
            return sems[name]

        ps = ctx.enter_context(nc.psum_tensor("ps", [P, 8, T], F32))
        bc_dram = nc.dram_tensor("bc_dram", (2, 2 * NS, NTOK), F32, kind="Internal").ap()

        ident = sb("ident", [P, P])
        spread = sb("spread", [P, NQ, P])
        fold = sb("fold", [P, 32])
        wT = sb("wT", [P, 16, P])
        gate_wT = sb("gate_wT", [DM, P])
        router_wT = sb("router_wT", [DM + 1, E])
        dtproj = sb("dtproj", [P, 2, P])
        skip = sb("skip", [P, 2, P])
        negA = sb("negA", [P, 2, NQ, NR])
        dt_b = sb("dt_b", [P, 2])
        conv_b = sb("conv_b", [P, 3])
        ln_g = sb("ln_g", [P, 1])
        ln_b = sb("ln_b", [P, 1])
        w1 = sb("w1", [DM, E, H])
        b1 = sb("b1", [P, NBLK])
        w2 = sb("w2", [P, NBLK, DM])
        b2 = sb("b2", [E, DM])
        pick = sb("pick", [E + 1, NBLK, P], BF16)
        rank = sb("rank", [P, E])
        carry = sb("carry", [P, 2, B, NQ, NR])
        lns = sb("lns", [P, 8, TB])
        x0 = sb("x0", [P, TILES, DM])
        gate = sb("gate", [P, NTOK])
        PADW = L + 3
        xs = sb("xs", [P, 2, B, PADW])
        z = sb("z", [P, 2, NTOK])
        ids = sb("ids", [TILES, P], I32)
        idx = sb("idx", [P, TILES], I32)
        ranki = sb("ranki", [P, E], I32)
        ohTb = sb("ohTb", [E + 1, T], BF16)
        arena = sb("arena", [P, ARENA])

        def carve(of, at, *shape, rows=P):
            n = int(np.prod(shape))
            v = of[0:rows, at:at + n]
            if len(shape) > 1:
                names = "abcd"[:len(shape)]
                v = v.rearrange(f"p ({' '.join(names)}) -> p {' '.join(names)}",
                                **{k: s for k, s in zip(names, shape)})
            return v, at + n

        uT, a = carve(arena, 0, B, L + 4)
        u2d, a = carve(arena, a, TILES, 2, DM)
        u, a = carve(arena, a, TB, DM)
        xc, a = carve(arena, a, TB, DM)
        sq, a = carve(arena, a, TB, DM)
        in_w, a = carve(arena, a, 2, DM)
        conv_w, a = carve(arena, a, 3, 4)
        dir_w, a = carve(arena, a, 2, 2, P)
        taps, a = carve(arena, a, 2, 2, DM)
        dir_taps, a = carve(arena, a, 2, 4, P)
        xbc, a = carve(arena, a, 2, P, rows=2 * NS)
        xdt, a = carve(arena, a, 2, P, rows=R)
        dt_w, a = carve(arena, a, 2, R)
        dskip, a = carve(arena, a, 2)
        dir_ow, a = carve(arena, a, 2, P)
        out_w, a = carve(arena, a, 4 * DM, rows=DM)
        router_w, a = carve(arena, a, DM, rows=E)
        alog, a = carve(arena, a, 2, NQ, NS)
        pickf, a = carve(arena, a, NBLK, P, rows=E + 1)
        idx_f, a = carve(arena, a, P, rows=TILES)
        idx_g, a = carve(arena, a, P, rows=TILES)
        dt_wT, a = carve(arena, a, 2, P, rows=R)
        assert a <= ARENA
        v_, a = carve(arena, 0, T)
        e_, a = carve(arena, a, T)
        w_, a = carve(arena, a, T)
        l_, a = carve(arena, a, T)
        dt, a = carve(arena, a, 2, T)
        du, a = carve(arena, a, 2, T)
        dbu, a = carve(arena, a, NR, T)
        hs, a = carve(arena, a, 2, NR, T)
        hc, a = carve(arena, a, 2, NR, T)
        rep, a = carve(arena, a, B, 2, NR, T)
        assert a <= ARENA
        EXTRA = 2 * T + 6 * TC * DM
        extra = sb("extra", [P, EXTRA])
        bc_sb, _ = carve(extra, 0, 2, T, rows=2 * NS)
        ga, a = carve(extra, 0, 2, T)
        h1, a = carve(extra, a, TC, DM)
        xf, a = carve(extra, a, TC, DM)
        fin, a = carve(extra, a, TC, DM)
        sq3, a = carve(extra, a, TC, DM)
        lg, a = carve(extra, a, TC, E)
        eq, a = carve(extra, a, TC, E)
        oh, a = carve(extra, a, TC, E)
        mx, a = carve(extra, a, TC)
        mx2, a = carve(extra, a, TC)
        assert a <= EXTRA
        xs0 = xs[:, 0].rearrange("p d w -> p (d w)")
        hid, a = carve(xs0, 0, NBLK, T)
        xfT, a = carve(xs0, a, B, T, rows=DM + 1)
        ohT, a = carve(xs0, a, T, rows=E)
        moeT = xs0[:, a - T:a - T // 2]
        h1b, a = carve(xs0, a, TC, DM)
        xc3, a = carve(xs0, a, TC, DM)
        assert a <= 2 * PADW

        last_ohTb = sb("last_ohTb", [E + 1, T], BF16)

        class Buffers:
            pass
        usual, last = Buffers(), Buffers()
        usual.ga, usual.h1, usual.h1b, usual.xc, usual.sq, usual.xf = ga, h1, h1b, xc3, sq3, xf
        usual.lg, usual.eq, usual.oh, usual.mx, usual.mx2 = lg, eq, oh, mx, mx2
        usual.fin, usual.hid, usual.ohT, usual.moeT, usual.ohTb = fin, hid, ohT, moeT, ohTb
        usual.xfT = (xfT[:, 0], xfT[:, 1])
        last.ga, a = carve(arena, 0, 2, T)
        last.h1, a = carve(arena, a, TC, DM)
        last.xc, a = carve(arena, a, TC, DM)
        last.sq, a = carve(arena, a, TC, DM)
        last.xf, a = carve(arena, a, TC, DM)
        last.fin, a = carve(arena, a, TC, DM)
        last.lg, a = carve(arena, a, TC, E)
        last.eq, a = carve(arena, a, TC, E)
        last.oh, a = carve(arena, a, TC, E)
        last.mx, a = carve(arena, a, TC)
        last.mx2, a = carve(arena, a, TC)
        last.hid, a = carve(arena, a, NBLK, T)
        last.ohT, a = carve(arena, a, T, rows=E)
        last.moeT, a = carve(arena, a, T // 2)
        one_xfT, a = carve(arena, a, T, rows=DM + 1)
        last.xfT = (one_xfT, one_xfT)
        last.h1b, last.ohTb = last.h1, last_ohTb
        assert a <= ARENA

        def conv_wT(d, k):
            return wT[:, 2 + 4 * d + k, :]

        def flat(ap):
            return ap.rearrange("p a b -> p (a b)")

        A = lambda n: ins["L0_attn_" + n]
        loads = []

        def load(dst, src):
            loads.append((dst, src))

        load(in_w, A("in_w").rearrange("(h c) j -> c h j", h=2))
        load(conv_w[:, 0, :], A("conv_w"))
        load(conv_b[:, 0:1], A("conv_b").rearrange("(c a) -> c a", a=1))
        for h in range(2):
            load(ln_g[DM * h:DM * h + DM], A("ln_g").rearrange("(c a) -> c a", a=1))
            load(ln_b[DM * h:DM * h + DM], A("ln_b").rearrange("(c a) -> c a", a=1))
        load(out_w, A("out_w"))
        for d, n in enumerate(DIRS):
            load(dir_w[:, d], A(n + "_in_w").rearrange("(h c) j -> c h j", h=2))
            load(conv_w[:, 1 + d, :], A(n + "_conv_w"))
            load(conv_b[:, 1 + d:2 + d], A(n + "_conv_b").rearrange("(c a) -> c a", a=1))
            load(xdt[:, d], A(n + "_xproj_w")[0:R, :])
            load(xbc[:, d], A(n + "_xproj_w")[R:R + 2 * NS, :])
            load(dt_w[:, d], A(n + "_dt_w"))
            load(dt_b[:, d:d + 1], A(n + "_dt_b").rearrange("(c a) -> c a", a=1))
            load(dskip[:, d:d + 1], A(n + "_D").rearrange("(c a) -> c a", a=1))
            load(dir_ow[:, d], A(n + "_out_w"))
            for m in range(4):
                load(alog[32 * m:32 * m + 32, d], A(n + "_Alog").rearrange("(q d) s -> d q s", d=32))
        F = lambda n: ins["L0_ffn_" + n]
        load(router_w, F("router_w"))
        EARLY_LOADS = len(loads)
        load(router_wT[DM:DM + 1, :], F("router_b").rearrange("(a e) -> a e", a=1))
        load(w1[:], F("W1").rearrange("e d h -> d e h"))
        load(b1[:], F("b1").rearrange("e h -> (e h)").rearrange("(n p) -> p n", p=P))
        load(w2[:], F("W2").rearrange("e h d -> (e h) d").rearrange("(n p) d -> p n d", p=P))
        load(b2[:], F("b2"))

        block = ctx.enter_context(nc.Block())
        NLN = 2 * B

        UPD = NCH

        PAIR = 2 * NQ * NR

        def bank(b, tile):
            return 3 + (NQ * NR * b + tile) % 3

        def bank_age(b, tile):
            at = NQ * NR * b + tile
            return next(n for n in range(1, PAIR) if (at - n) % PAIR % 3 == at % 3)

        SIDE, SIDE2 = 2, 7
        FORWARD = 6

        def xs_at(d, i, b, shift=0):
            return xs[:, d, b, bass.ds((i - CB * d) * T + shift, T)]

        def z_at(d, i, b):
            return z[:, d, bass.ds((i - CB * d) * T + b * L, T)]

        def follows(d, i, b):
            if b == 0:
                return d, i, 1
            return (1 if isinstance(i, int) and i == CB - 1 else d), i + 1, 0

        def is_unit(i, b, *units):
            return isinstance(i, int) and 2 * i + b in units

        def a2_items(i, b):
            u = 2 * i + b
            if isinstance(i, int) and i == CB - 1:
                return [(u + UPD, 1, i + CB, b)]
            return [(u * 2 + 2, 0, i + 1, b), (u * 2 + 3, 1, i + CB, b)]

        def a2_before(i, b):
            if is_unit(i, b, 0):
                return None
            pi, pb = (i, 0) if b else (i - 1, 1)
            m = (pi * 2 + pb) + UPD if isinstance(pi, int) and pi == CB - 1 else (pi * 2 + pb) * 2 + 3
            return m, 1, pi + CB, pb

        def forward_before(d, i, b):
            if is_unit(i, b, 0) or (d and not is_unit(i, b, UPD)):
                return None
            return (2 * i, i * T) if b else (i * 2 - 1, i * T + (L - T))

        def c_chunk(i, b, lag):
            bb = (b + lag) % 2
            j = i - CB - (lag - b + 1) // 2
            m = j * 2 + bb
            return None if isinstance(m, int) and not 0 <= m < NCH else (m, j, bb)

        def tokens(j, bb):
            return j * -1 + (CB * bb + CB - 1)

        M = NCH - 1
        usual.side, usual.side2, usual.moe = SIDE, SIDE2, SIDE
        last.side, last.side2, last.moe = 5, 4, 3

        def hidden_bank(m, k):
            banks = {M - 2: (SIDE, 0, 1, 3), M - 1: (SIDE, 6, SIDE2, 3), M: (5, 4, 0, 1)}
            return banks[m][k] if isinstance(m, int) and m in banks else SIDE

        def is_last(m):
            return isinstance(m, int) and m == NCH - 1

        def buffers(m):
            return last if is_last(m) else usual

        END, MIDDLE, FRONT = 3, 2, 1
        TAIL = [(FRONT, M, 5), (MIDDLE, M - 1, 0), (MIDDLE, M - 1, 1), (END, M - 2, 0), (FRONT, M, 7),
                (END, M - 2, 1), (END, M - 2, 2), (MIDDLE, M - 1, 3), (END, M - 2, 3), (MIDDLE, M, 0),
                (MIDDLE, M - 1, 4), (MIDDLE, M, 1), (END, M - 2, 4), (MIDDLE, M, 3), (MIDDLE, M - 1, 5),
                (END, M - 2, 5), (MIDDLE, M, 4), (END, M - 2, 6), (MIDDLE, M - 1, 6), (MIDDLE, M - 1, 7),
                (MIDDLE, M, 5), (END, M - 1, 0), (END, M - 1, 1), (MIDDLE, M, 7), (END, M - 1, 2),
                (END, M - 1, 3), (END, M, 0), (END, M, 1), (END, M - 1, 4), (END, M, 2), (END, M, 3),
                (END, M - 1, 5), (END, M, 4), (END, M - 1, 6), (END, M, 5), (END, M, 6)]

        def tail(steps):
            for lag, m, s in TAIL:
                if lag in steps:
                    steps[lag](s, m, m // 2, m % 2)

        def wait(eng, name, value):
            if not (isinstance(value, int) and value <= 0):
                eng.wait_ge(sem(name), value)

        def units(eng, unit, loop=None):
            for b in range(2):
                unit(0, 0, b)
            with eng.Fori(1, CB - 1) as i:
                for b in range(2):
                    unit(0, i, b)
            for b in range(2):
                unit(0, CB - 1, b)
            unit(1, CB, 0)
            unit(1, CB, 1)
            unit(1, CB + 1, 0)

            def body(i):
                unit(1, i, 1)
                unit(1, i + 1, 0)
            if loop:
                loop(CB + 1, NCH - 1, body)
            else:
                with eng.Fori(CB + 1, NCH - 1) as i:
                    body(i)
            unit(1, NCH - 1, 1)

        @block.sync
        def _(sp):
            sp.dma_start(ids[:], x.rearrange("b (t p) -> (b t) p", p=P)).then_inc(sem("ids_in"), 16)
            with nc.allow_non_contiguous_dma(reason="b1 is 2 KB"):
                for dst, src in loads[0:EARLY_LOADS:2]:
                    sp.dma_start(dst, src).then_inc(sem("weights_in"), 16)
                for dst, src in loads[EARLY_LOADS:]:
                    sp.dma_start(dst, src).then_inc(sem("c_weights_in"), 16)

            def store_bc(item, d, i, b):
                k = b if isinstance(i, int) and i == 0 else d
                to = bc_dram[d, :, bass.ds(i * T + (b * L - CB * d * T), T)]
                sp.wait_ge(sem("bc_in_sbuf"), item + 1)
                sp.dma_start(to, bc_sb[:, k, :]) \
                  .then_inc(sem(f"bc_in_dram_{k}"), 16)

            def load_rep(d, i, b):
                rows = bc_dram[d].rearrange("(k m) t -> m k t", m=4).unsqueeze(1) \
                                 .broadcast_to([4, 32, 2 * NR, NTOK])[:, :, :, bass.ds(i * T + (b * L - CB * d * T), T)]
                if isinstance(i, int) and i == 0:
                    k, count = b, 1
                else:
                    k, count = d, i * 2 + (b + 2 * d - 2 * CB * d)
                if not (isinstance(i, int) and i == 0):
                    sp.wait_ge(sem("hc_ready"), i * (2 * NQ) + (b - 1) * NQ)
                sp.wait_ge(sem(f"bc_in_dram_{k}"), count * 16)
                for m in range(4):
                    sp.dma_start(rep[32 * m:32 * m + 32, b].rearrange("p a b t -> p (a b) t"), rows[m]) \
                      .then_inc(sem(f"rep_in_{b}"), 16)

            def store(m, j, bb):
                to = out.rearrange("b (t p) d -> p (b t) d", p=P)[:, bass.ds(tokens(j, bb) * TC, TC), :]
                sp.wait_ge(sem("fin_ready"), m + 2)
                sp.dma_start(to, buffers(m).fin) \
                  .then_inc(sem("out_done"), 16)

            for b in range(2):
                store_bc(b, 0, 0, b)
                load_rep(0, 0, b)

            def unit(d, i, b):
                if not is_unit(i, b, 0, UNITS - 1):
                    load_rep(*follows(d, i, b))
                if d == 0 or is_unit(i, b, UPD):
                    if a2_before(i, b):
                        store_bc(*a2_before(i, b))
                if d == 0 and not (isinstance(i, int) and i == CB - 1):
                    store_bc(*a2_items(i, b)[0])
                if d and c_chunk(i, b, 3):
                    store(*c_chunk(i, b, 3))

            units(sp, unit)
            for i, b in ((NCH, 0), (NCH, 1), (NCH + 1, 0)):
                store(*c_chunk(i, b, 3))
            sp.wait_ge(sem("out_done"), 16 * (NCH + 1))

        @block.gpsimd
        def _(pool):
            ch = Chain(pool, sem("pool_step"))

            def fill_where(view, pattern, base, fill):
                ch.step(pool.affine_select(out=view, in_=view, compare_op=ALU.not_equal, fill=fill,
                                           base=base, pattern=pattern, channel_multiplier=1))

            ch.step(pool.memset(ident[:], 0.0))
            fill_where(ident[:], [[-1, P]], 0, 1.0)
            pool.memset(fold[:], 0.0).then_inc(sem("ident_ready"), 1)
            pool.wait_ge(sem("ident_ready"), 1)
            for m in range(4):
                fill_where(fold[:], [[-1, 32]], -32 * m, 1.0)
            ch.step(pool.memset(pickf, 0.0))
            fill_where(pickf.rearrange("p n (e h) -> p n e h", h=H),
                       [[-(P // H), NBLK], [-1, P // H], [0, H]], 0, BIG)
            ch.step(pool.memset(pickf[E:E + 1], -BIG))
            ch.step(pool.iota(ranki[:], pattern=[[-1, E]], base=E, channel_multiplier=0))
            pool.memset(lns[:], 0.0).then_inc(sem("consts"), 1)

            rows = table.rearrange("v (s d) -> (v s) d", d=DM)
            pool.wait_ge(sem("idx_ready"), 1)
            for t in range(TILES):
                pool.indirect_dma_start(
                    out=x0[:, t, :], out_offset=None, in_=rows,
                    in_offset=bass.IndirectOffsetOnAxis(ap=idx[:, t:t + 1], axis=0),
                ).then_inc(sem(f"gathered_{t // TB}"), 16)

            def softplus(unit, b):
                pool.wait_ge(sem("sp_c"), unit + 1)
                pool.tensor_tensor(l_, l_, e_, ALU.subtract).then_inc(sem("sp_log1p"), 1)
                pool.wait_ge(sem("sp_log1p"), unit + 1)
                pool.tensor_tensor(dt[:, b], v_, l_, ALU.add).then_inc(sem("dt_ready"), 1)

            def by_c(i, b, q):
                done = (2 * i + b) * NQ + q
                if q == 0:
                    pool.wait_ge(sem(f"rep_in_{b}"), i * 64 + 64)
                if not (is_unit(i, b, 0) and q < 2):
                    pool.wait_ge(sem("summed"), done - 1)
                pool.wait_ge(sem("scans"), done * NR + NR)
                pool.tensor_tensor(flat(hc[:, q % 2]), flat(hs[:, q % 2]), flat(rep[:, b, 1]), ALU.mult) \
                    .then_inc(sem("hc_ready"), 1)

            def unit(d, i, b):
                for q in range(NQ):
                    by_c(i, b, q)
                    if q == 0 and not is_unit(i, b, UNITS - 1):
                        softplus(2 * i + b + 1, 1 - b)

            softplus(0, 0)
            units(pool, unit)

        @block.tensor
        def _(pe):
            pe.wait_ge(sem("ident_ready"), 1)
            pe.wait_ge(sem("ids_clamped"), 1)
            pe.transpose(ps[:, 6, 0:TILES], idx_f, ident[0:TILES, 0:TILES]).then_inc(sem("idx_ps"), 1)

            pe.wait_ge(sem("weights_in"), 16 * EARLY_LOADS)
            pe.wait_ge(sem("taps_ready"), 1)

            def turn(slot, src, at=0):
                k, m = src.shape[0], src.shape[1]
                return pe.transpose(ps[0:m, slot // 4, (slot % 4) * P + at:(slot % 4) * P + at + k],
                                    src, ident[0:k, 0:k])

            for s in range(2):
                turn(s, flat(taps[:, s]))
            for d in range(2):
                for k in range(4):
                    turn(2 + 4 * d + k, dir_taps[:, d, k])
            for d in range(2):
                turn(10 + d, dir_w[:, d, 1])
                turn(12 + d, dir_ow[:, d])
                turn(14, out_w[:, P * d:P * d + P], at=DM * d)
                turn(15, xbc[:, d], at=2 * NS * d)
            turn(16, in_w[:, 1])
            turn(17, router_w)
            for d in range(2):
                mm = turn(18 + d, dt_w[:, d])
            mm.then_inc(sem("wT_ps"), 1)
            pe.wait_ge(sem("wT_copied"), 8)
            for d in range(2):
                mm = pe.matmul(ps[:, 5, P * d:P * d + P], xdt[:, d], dt_wT[:, d], start=True, stop=True)
            mm.then_inc(sem("dtproj_ps"), 1)
            pe.wait_ge(sem("wT_copied"), 9)

            def turn_chunk(b, c):
                n = CB * b + c
                if c == 0:
                    pe.wait_ge(sem("u2_ready"), b + 1)
                if n >= 2:
                    pe.wait_ge(sem("uT_ready"), 2 * n - 2)
                for t in range(TC):
                    tr = pe.transpose(ps[:, c % 2, t * P:t * P + P], flat(u2d[:, TB * b + TC * c + t]), ident[:])
                tr.then_inc(sem("turned"), 1)

            def project_chunk(b, c):
                n = CB * b + c
                pe.wait_ge(sem("uT_ready"), 2 * n + 2)
                if n >= 2:
                    pe.wait_ge(sem("act_r_ready"), n - 1)
                    pe.wait_ge(sem("gate_ready"), n - 1)
                for s in range(2):
                    mm = pe.matmul(ps[:, 2 + c % 2, :], wT[:, s, :],
                                   uT[:, b, c * T + 3 - 2 * s:c * T + 3 - 2 * s + T],
                                   start=(s == 0), stop=(s == 1))
                mm.then_inc(sem("x_ps"), 1)
                pe.matmul(ps[:, 4 + c % 2, :], gate_wT[:], uT[0:DM, b, c * T + 3:c * T + 3 + T],
                          start=True, stop=True).then_inc(sem("gate_ps"), 1)

            def a2_conv(part, m, d, i, b):
                if part == 0:
                    wait(pe, "bc_in_sbuf", m)
                for k in range(2 * part, 2 * part + 2):
                    mm = pe.matmul(ps[:, SIDE, :], conv_wT(d, k), xs_at(d, i, b, k),
                                   start=(k == 0), stop=(k == 3))
                if part == 1:
                    mm.then_inc(sem("xs_ps"), 1)

            def a2_z(m, d, i, b, free):
                wait(pe, *free)
                pe.matmul(ps[:, SIDE2, :], wT[:, 10 + d, :], xs_at(d, i, b, 3),
                          start=True, stop=True).then_inc(sem("z_ps"), 1)

            def a2_bc(m, d, i, b):
                pe.wait_ge(sem("xs_ready"), m + 1)
                pe.matmul(ps[:, SIDE, :], wT[:, 15, :],
                          xs_at(d, i, b), start=True, stop=True).then_inc(sem("bc_ps"), 1)

            def a2_first(b):
                pe.wait_ge(sem("act_r_ready"), CB * b + CB - 1)
                a2_conv(0, b, 0, 0, b)
                a2_conv(1, b, 0, 0, b)
                a2_z(b, 0, 0, b, ("softplus_a", b))

            turn_chunk(0, 0)
            for n in range(NCH):
                if n + 1 < NCH and n != CB - 1:
                    turn_chunk((n + 1) // CB, (n + 1) % CB)
                project_chunk(n // CB, n % CB)
                if n == CB - 1:
                    a2_first(0)
                    a2_bc(0, 0, 0, 0)
                    turn_chunk(1, 0)
                    pe.wait_ge(sem("bc_in_sbuf"), 1)

            def pre(d, i, b, free):
                wait(pe, *free)
                pe.matmul(ps[:, SIDE2, :], dtproj[:, d, :], xs_at(d, i, b), start=True, stop=True) \
                  .then_inc(sem("pre_ps"), 1)

            def spread_du(i, b, q):
                done = (2 * i + b) * NQ + q
                if q == 0:
                    pe.wait_ge(sem("du_ready"), 2 * i + b + 1)
                wait(pe, "dbu_ready", done)
                pe.matmul(ps[:, 1, :], spread[:, q, :], du[:, b], start=True, stop=True) \
                  .then_inc(sem("du_spread"), 1)

            def spread_dt(i, b, q):
                done = (2 * i + b) * NQ + q
                if q == 0:
                    pe.wait_ge(sem("dt_ready"), 2 * i + b + 1)
                wait(pe, "decay_ready", done * NR)
                pe.matmul(ps[:, 0, :], spread[:, q, :], dt[:, b], start=True, stop=True) \
                  .then_inc(sem("dt_spread"), 1)

            def nsum(d, i, b, q):
                if q == 0:
                    wait(pe, "yz_ready", 2 * i + b)
                    pe.matmul(ps[:, 6, :], skip[:, d, :], xs_at(d, i, b),
                              start=True, stop=False, skip_group_check=True)
                pe.wait_ge(sem("hc_ready"), (2 * i + b) * NQ + q + 1)
                for r in range(NR):
                    mm = pe.matmul(ps[32 * q:32 * q + 32, 6, :], fold[:], hc[:, q % 2, r],
                                   start=False, stop=(r == NR - 1), skip_group_check=True)
                mm.then_inc(sem("summed"), 1)

            def c_front(s, m, j, bb):
                c = buffers(m)
                if s == 5:
                    if not is_last(m):
                        wait(pe, "logits_read", m)
                    pe.wait_ge(sem("yz_ready"), m + UPD + 1)
                    pe.matmul(ps[:, c.side2, :], wT[:, 13, :], z[:, 1, bass.ds(j * T + bb * L, T)],
                              start=True, stop=True).then_inc(sem("dir_out"), 1)
                if s == 7:
                    pe.wait_ge(sem("ga_forward"), m + 1)
                    pe.wait_ge(sem("ga_backward"), m + 1)
                    for t in range(TC):
                        for d in range(2):
                            mm = pe.matmul(ps[:, c.side2, t * DM:t * DM + DM], c.ga[:, d, t * P:t * P + P],
                                           wT[:, 14, DM * d:DM * d + DM], start=(d == 0), stop=(d == 1))
                    mm.then_inc(sem("attn_ps"), 1)

            def c_middle(s, m, j, bb):
                c = buffers(m)
                if s == 3:
                    pe.wait_ge(sem("softplus_a"), m + UPD + 4 if not isinstance(m, int) else min(m + UPD + 4, UNITS))
                    pe.wait_ge(sem("xf_ready"), m + 1)
                    for h in range(TC // 2):
                        tr = pe.transpose(ps[:, c.side2, h * P:h * P + P], flat(c.xf[:, 2 * h:2 * h + 2]), ident[:])
                    tr.then_inc(sem("xfT_ps"), 1)
                if s == 4:
                    pe.wait_ge(sem("xfT_ready"), m * 2 + 2)
                    for t in range(TC):
                        mm = pe.matmul(ps[:, c.side2, t * E:t * E + E], c.xfT[bb][:, t * P:t * P + P], router_wT[:],
                                       start=True, stop=True)
                    mm.then_inc(sem("logits_ps"), 1)
                if s == 7:
                    pe.wait_ge(sem("choice_ready"), m + 1)
                    if not is_last(m):
                        pe.wait_ge(sem("fin_ready"), m + 1)
                    for t in range(TC):
                        tr = pe.transpose(ps[0:E, c.side, t * P:t * P + P], c.oh[:, t], ident[:])
                    tr.then_inc(sem("choice_ps"), 1)

            def c_end(s, m, j, bb):
                c = buffers(m)
                if s < NBLK:
                    if s == 0:
                        pe.wait_ge(sem("choiceT"), m + 1)
                        pe.wait_ge(sem("choiceT_bf16"), m + 1)
                    elif hidden_bank(m, s) == SIDE:
                        pe.wait_ge(sem("hidden"), m * NBLK + s)
                    bank = hidden_bank(m, s)
                    pe.matmul(ps[:, bank, :], pick[:, s, :], c.ohTb[:], start=True, stop=False)
                    pe.matmul(ps[:, bank, :], w1[:, 8 * s:8 * s + 8, :].rearrange("p e h -> p (e h)"),
                              c.xfT[bb][0:DM, :], start=False, stop=True).then_inc(sem("hidden_ps"), 1)
                if s == 4:
                    pe.wait_ge(sem("hidden"), m * NBLK + NBLK)
                if s in (4, 5):
                    for h in range(2):
                        y, half = ps[DM * h:DM * h + DM, c.moe, 0:T // 2], slice(h * T // 2, (h + 1) * T // 2)
                        for k in (0, 1) if s == 4 else (2, 3):
                            pe.matmul(y, w2[:, k, :], c.hid[:, k, half], start=(k == 0), stop=False,
                                      skip_group_check=True)
                        if s == 5:
                            mm = pe.matmul(y, b2[:], c.ohT[:, half], start=False, stop=True, skip_group_check=True)
                if s == 5:
                    mm.then_inc(sem("moe_ps"), 1)
                if s == 6:
                    pe.wait_ge(sem("moe_relu"), m + 1)
                    for g in range(TC // 2):
                        tr = pe.transpose(ps[:, c.moe, g * P:g * P + P], c.moeT[:, g * P:g * P + P], ident[:])
                    tr.then_inc(sem("moe_turned"), 1)

            def c_slot(i, b, s):
                for lag, step in ((3, c_end), (2, c_middle), (1, c_front)):
                    if c_chunk(i, b, lag):
                        step(s, *c_chunk(i, b, lag))

            def unit(d, i, b):
                for s in range(2 * NQ):
                    q = s // 2
                    if s % 2 == 0:
                        spread_du(i, b, q)
                    else:
                        spread_dt(i, b, q)
                        if d:
                            c_slot(i, b, s - 1)
                        if s == 5 and d == 0 and len(a2_items(i, b)) == 2:
                            a2_bc(*a2_items(i, b)[0])
                        if q >= 2:
                            nsum(d, i, b, q - 2)
                        elif b:
                            nsum(d, i, 0, q + 2)
                        elif not is_unit(i, b, 0):
                            nsum(0 if is_unit(i, b, UPD) else d, i - 1, 1, q + 2)
                    if s == 1 and (d == 0 or is_unit(i, b, UPD)) and a2_before(i, b):
                        a2_bc(*a2_before(i, b))
                    if s == 1 and not is_unit(i, b, UNITS - 1):
                        if d == 0:
                            free = ("z_ready", a2_items(i, b)[0][0])
                        elif is_unit(i, b, UPD):
                            free = ("z_ready", 2 * UPD)
                        elif is_unit(i, b, UPD + 1):
                            free = ("forward_gated", UPD)
                        else:
                            free = ("h1_sum", (i - CB) * 2 + b - 1)
                        pre(*follows(d, i, b), free)
                    if s == FORWARD and forward_before(d, i, b):
                        m, at = forward_before(d, i, b)
                        if is_unit(i, b, UPD - 2, UPD - 1, UPD):
                            pe.wait_ge(sem("softplus_a"), 2 * i + b + 2)
                        else:
                            pe.wait_ge(sem("z_ready"), a2_items(i, b)[0][0] + 1)
                        pe.wait_ge(sem("yz_ready"), m + 1)
                        pe.matmul(ps[:, SIDE2, :], wT[:, 12, :], z[:, 0, bass.ds(at, T)],
                                  start=True, stop=True).then_inc(sem("forward_out"), 1)
                    if d == 0:
                        items = a2_items(i, b)
                        read = ("softplus_a", 2 * i + b + 2)
                        if len(items) == 2:
                            if s == 2:
                                a2_conv(0, *items[0])
                            if s == 3:
                                a2_conv(1, *items[0])
                                a2_z(*items[0], read)
                        if s == 6:
                            a2_conv(0, *items[-1])
                        if s == 7:
                            a2_conv(1, *items[-1])
                            gated = ("z_ready", items[-1][0]) if is_unit(i, b, 0) else ("forward_gated", 2 * i + b)
                            a2_z(*items[-1], gated)
                    if d and s % 2:
                        c_slot(i, b, s)

            pe.wait_ge(sem("constants_ready"), 1)
            pre(0, 0, 0, ("z_ready", 1))
            a2_first(1)
            a2_bc(1, 0, 0, 1)
            units(pe, unit)
            nsum(1, NCH - 1, 1, 2)
            nsum(1, NCH - 1, 1, 3)
            tail({END: c_end, MIDDLE: c_middle, FRONT: c_front})

        @block.scalar
        def _(act_e):
            def ln_rsqrt(ordinal, width):
                act_e.wait_ge(sem("ln_var"), ordinal)
                act_e.activation(lns[:, 2, 0:width], lns[:, 4, 0:width], ACT.Ln).then_inc(sem("ln_log"), 1)
                act_e.wait_ge(sem("ln_log"), ordinal)
                act_e.activation(lns[:, 3, 0:width], lns[:, 2, 0:width], ACT.Exp, scale=-0.5) \
                     .then_inc(sem("ln_rsqrt"), 1)

            def exp_ln_tables():
                act_e.preload_act_table_set("natural_log_exp_and_others")

            with nc.allow_non_contiguous_dma(reason="b1 is 2 KB"):
                for dst, src in loads[1:EARLY_LOADS:2]:
                    act_e.dma_start(dst, src).then_inc(sem("weights_in"), 16)
            exp_ln_tables()
            act_e.wait_ge(sem("weights_in"), 16 * EARLY_LOADS)
            for m in range(4):
                rows = slice(32 * m, 32 * m + 32)
                act_e.activation(negA[rows].rearrange("p a b c -> p (a b) c"),
                                 alog[rows].rearrange("p a b (r m) -> p (a b) r m", m=4)[:, :, :, m],
                                 ACT.Exp).then_inc(sem("expA"), 1)
            act_e.wait_ge(sem("wT_ps"), 1)
            act_e.wait_ge(sem("pads_ready"), 1)

            def out_of_psum(dst, src, name="wT_copied"):
                act_e.activation(dst, src, ACT.Copy).then_inc(sem(name), 1)

            for k in range(3):
                out_of_psum(flat(wT[:, 4 * k:4 * k + 4, :]), ps[:, k, :])
            out_of_psum(flat(wT[:, 12:15, :]), ps[:, 3, 0:3 * P])
            out_of_psum(wT[:, 15, 0:4 * NS], ps[:, 3, 3 * P:3 * P + 4 * NS])
            out_of_psum(gate_wT[:], ps[0:DM, 4, 0:P])
            out_of_psum(router_wT[0:DM, :], ps[0:DM, 4, P:P + E])
            out_of_psum(flat(dt_wT), ps[0:R, 4, 2 * P:4 * P])
            act_e.wait_ge(sem("dtproj_ps"), 1)
            out_of_psum(flat(dtproj[:]), ps[:, 5, 0:2 * P])

            def uT_chunk(b, c):
                n, at = CB * b + c, c * T
                act_e.wait_ge(sem("turned"), n + 1)
                for h in range(2):
                    rows = slice(DM * h, DM * h + DM)
                    act_e.activation(uT[rows, b, at + 3 + h:at + 3 + h + T], ps[rows, c % 2, :], ACT.Identity,
                                     scale=ln_g[rows, 0:1], bias=ln_b[rows, 0:1]).then_inc(sem("uT_ready"), 1)

            def a1_silus(b, c):
                n, at = CB * b + c, c * T
                act_e.wait_ge(sem("x_ps"), n + 1)
                act_e.activation(xs[:, 0, b, at + 3:at + 3 + T], ps[:, 2 + c % 2, :], ACT.Silu,
                                 bias=conv_b[:, 0:1]).then_inc(sem("act_ready"), 1)
                act_e.activation(xs[:, 1, b, L - T + 3 - at:L + 3 - at], ps[:, 2 + c % 2, REV], ACT.Silu,
                                 bias=conv_b[:, 0:1]).then_inc(sem("act_r_ready"), 1)
                act_e.wait_ge(sem("gate_ps"), n + 1)
                act_e.activation(gate[:, n * T:n * T + T], ps[:, 4 + c % 2, :], ACT.Silu) \
                     .then_inc(sem("gate_ready"), 1)

            def a2_silus(m, d, i, b):
                act_e.wait_ge(sem("xs_ps"), m + 1)
                act_e.wait_ge(sem("z_ps"), m + 1)
                act_e.activation(xs_at(d, i, b), ps[:, SIDE, :], ACT.Silu,
                                 bias=conv_b[:, 1 + d:2 + d]).then_inc(sem("xs_ready"), 1)
                act_e.activation(z_at(d, i, b), ps[:, SIDE2, :], ACT.Silu) \
                     .then_inc(sem("z_ready"), 1)

            ln_rsqrt(1, TB)
            ln_rsqrt(2, TB)
            uT_chunk(0, 0)
            def bc_out(b):
                act_e.wait_ge(sem("bc_ps"), b + 1)
                act_e.activation(bc_sb[:, b, :], ps[0:2 * NS, SIDE, :], ACT.Copy).then_inc(sem("bc_in_sbuf"), 1)

            for n in range(NCH):
                if n + 1 < NCH and n != CB - 1:
                    uT_chunk((n + 1) // CB, (n + 1) % CB)
                a1_silus(n // CB, n % CB)
                if n in (0, 2):
                    exp_ln_tables()
                    ln_rsqrt(3 + n // 2, TB)
                if n == CB - 1:
                    a2_silus(0, 0, 0, 0)
                    bc_out(0)
                    uT_chunk(1, 0)
            exp_ln_tables()

            def softplus(d, i, b, first=False):
                unit = 2 * i + b
                if not first:
                    act_e.wait_ge(sem("dt_ready"), unit)
                act_e.wait_ge(sem("pre_ps"), unit + 1)
                act_e.activation(v_, ps[:, SIDE2, :], ACT.Relu, bias=dt_b[:, d:d + 1])
                act_e.activation(w_, ps[:, SIDE2, :], ACT.Abs, bias=dt_b[:, d:d + 1]).then_inc(sem("softplus_a"), 1)
                act_e.wait_ge(sem("softplus_a"), unit + 1)
                act_e.activation(e_, w_, ACT.Exp, scale=-1.0).then_inc(sem("softplus_e"), 1)
                act_e.wait_ge(sem("softplus_e"), unit + 1)
                act_e.activation(w_, e_, ACT.Identity, bias=1.0).then_inc(sem("softplus_w"), 1)
                act_e.wait_ge(sem("softplus_w"), unit + 1)
                act_e.activation(l_, w_, ACT.Ln).then_inc(sem("softplus_l"), 1)

            def decays(d, i, b, q, half):
                done = (2 * i + b) * NQ + q
                if half == 0:
                    act_e.wait_ge(sem("dt_spread"), done + 1)
                for r in range(2 * half, 2 * half + 2):
                    tile = NR * q + r
                    if not (is_unit(i, b, 0) and tile < 3):
                        act_e.wait_ge(sem("scans"), done * NR + r + 1 - bank_age(b, tile))
                    act_e.activation(ps[:, bank(b, tile), :], ps[:, 0, :], ACT.Exp,
                                     scale=negA[:, d, q, r:r + 1]).then_inc(sem("decay_ready"), 1)

            def c_middle(s, m, j, bb):
                c = buffers(m)
                if s == 0:
                    ln_rsqrt(m + (NLN + 1), TC)
                if s == 3:
                    act_e.wait_ge(sem("xfT_ps"), m + 1)
                    for h in range(2):
                        act_e.activation(
                            c.xfT[bb][0:DM, :].rearrange("p (g h t) -> p g h t", h=2, t=P)[:, :, h],
                            ps[DM * h:DM * h + DM, c.side2, 0:T // 2].rearrange("p (g t) -> p g t", t=P),
                            ACT.Copy).then_inc(sem("xfT_ready"), 1)
                if s == 4:
                    act_e.wait_ge(sem("logits_ps"), m + 1)
                    wait(act_e, "choice_ready", m)
                    act_e.activation(flat(c.lg), ps[:, c.side2, 0:TC * E], ACT.Copy).then_inc(sem("logits_read"), 1)
                if s == 7:
                    act_e.wait_ge(sem("choice_ps"), m + 1)
                    act_e.activation(c.ohT, ps[0:E, c.side, :], ACT.Copy).then_inc(sem("choiceT"), 1)
                    act_e.activation(c.ohTb[0:E, :], ps[0:E, c.side, :], ACT.Copy).then_inc(sem("choiceT_bf16"), 1)

            def c_end(s, m, j, bb):
                c = buffers(m)
                if s < NBLK:
                    act_e.wait_ge(sem("hidden_ps"), m * NBLK + s + 1)
                    act_e.activation(c.hid[:, s, :], ps[:, hidden_bank(m, s), :], ACT.Relu, bias=b1[:, s:s + 1]) \
                         .then_inc(sem("hidden"), 1)
                if s == 5:
                    act_e.wait_ge(sem("moe_ps"), m + 1)
                    act_e.activation(c.moeT, ps[:, c.moe, 0:T // 2], ACT.Relu).then_inc(sem("moe_relu"), 1)

            def c_front(s, m, j, bb):
                c = buffers(m)
                if s == 5:
                    if isinstance(m, int) and m == 0:
                        act_e.wait_ge(sem("forward_gated"), UPD)
                        act_e.wait_ge(sem("bc_in_dram_0"), 16 * (NCH - 1))
                    else:
                        act_e.wait_ge(sem("attn_ps"), m)
                    act_e.activation(c.ga[:, 0], z[:, 0, bass.ds(tokens(j, bb) * T, T)], ACT.Copy) \
                         .then_inc(sem("ga_forward"), 1)

            def c_slot(i, b, s):
                for lag, step in ((3, c_end), (2, c_middle), (1, c_front)):
                    if c_chunk(i, b, lag):
                        step(s, *c_chunk(i, b, lag))

            EARLY = (1, 2, 3, 4)

            def unit(d, i, b):
                for s in range(2 * NQ):
                    early = d and s in EARLY
                    if early:
                        c_slot(i, b, s)
                    decays(d, i, b, s // 2, s % 2)
                    if s == 1 and not is_unit(i, b, UNITS - 1):
                        softplus(*follows(d, i, b))
                    if d == 0:
                        items = a2_items(i, b)
                        if s == 3 and len(items) == 2:
                            a2_silus(*items[0])
                            exp_ln_tables()
                        if s == 7:
                            a2_silus(*items[-1])
                            exp_ln_tables()
                    elif not early:
                        c_slot(i, b, s)

            act_e.wait_ge(sem("constants_ready"), 1)
            softplus(0, 0, 0, first=True)
            a2_silus(1, 0, 0, 1)
            bc_out(1)
            exp_ln_tables()
            units(act_e, unit)
            act_e.wait_ge(sem("yz_ready"), UNITS)
            tail({END: c_end, MIDDLE: c_middle, FRONT: c_front})

        @block.vector
        def _(dve):
            ch = Chain(dve, sem("dve_step"))

            dve.wait_ge(sem("ids_in"), 16)
            ch.step(dve.tensor_copy(idx_f, ids[:]))
            ch.step(dve.tensor_scalar(idx_g, idx_f, 0.0, float(V), ALU.is_lt, ALU.mult))
            ch.step(dve.tensor_tensor(idx_g, idx_g, idx_f, ALU.add))
            ch.step(dve.tensor_scalar(idx_g, idx_g, 0.0, float(V - 1), ALU.max, ALU.min))
            dve.tensor_scalar(idx_f, idx_g, float(HID // DM), float(SLICE), ALU.mult, ALU.add) \
               .then_inc(sem("ids_clamped"), 1)
            dve.wait_ge(sem("idx_ps"), 1)
            dve.tensor_copy(idx[:], ps[:, 6, 0:TILES]).then_inc(sem("idx_ready"), 1)

            dve.wait_ge(sem("consts"), 1)
            ch.mark(dve.memset(last_ohTb[E:E + 1, :], 1.0))
            ch.mark(dve.tensor_copy(rank[:], ranki[:]))
            ch.mark(dve.tensor_copy(pick[:], pickf))
            dve.wait_ge(sem("weights_in"), 16 * EARLY_LOADS)
            for k in range(4):
                ch.mark(dve.tensor_scalar(taps[:, (3 - k) // 2, (3 - k) % 2, :], in_w[:, 0, :],
                                          conv_w[:, 0, k:k + 1], None, ALU.mult))
                for d in range(2):
                    ch.mark(dve.tensor_scalar(dir_taps[:, d, k, :], dir_w[:, d, 0, :],
                                              conv_w[:, 1 + d, k:k + 1], None, ALU.mult))
            ch.wait()
            dve.tensor_copy(spread[:].rearrange("p q (n d) -> p q n d", d=32),
                            ident[:].rearrange("p (q d) -> p q d", d=32).unsqueeze(2)
                            .broadcast_to([P, NQ, 4, 32])).then_inc(sem("taps_ready"), 1)
            ch.mark(dve.memset(wT[:, 15, 4 * NS:], 0.0))
            ch.mark(dve.memset(xs[:, :, :, 0:3], 0.0))
            ch.mark(dve.memset(carry[:].rearrange("p a b c d -> p (a b c d)"), 0.0))
            ch.wait()
            dve.memset(uT[:, :, 0:4], 0.0).then_inc(sem("pads_ready"), 1)

            def ln_centre(src, xc, sq, width):
                mean, total, var = (lns[:, k, 0:width] for k in (0, 1, 4))
                ch.step(dve.tensor_reduce(mean, src, AX, ALU.add))
                ch.step(dve.tensor_scalar(mean, mean, 1.0 / DM, None, ALU.mult))
                ch.step(dve.tensor_tensor(xc, src, mean.unsqueeze(2).broadcast_to([P, width, DM]), ALU.subtract))
                ch.step(dve.tensor_tensor(sq, xc, xc, ALU.mult))
                ch.step(dve.tensor_reduce(total, sq, AX, ALU.add))
                dve.tensor_scalar(var, total, 1.0 / DM, EPS, ALU.mult, ALU.add).then_inc(sem("ln_var"), 1)

            def ln_scale(ordinal, xc, width, outs):
                dve.wait_ge(sem("ln_rsqrt"), ordinal)
                r, var, t, y = (lns[:, k, 0:width] for k in (3, 4, 5, 6))
                ch.step(dve.tensor_tensor(t, r, r, ALU.mult))
                ch.step(dve.tensor_tensor(t, t, var, ALU.mult))
                ch.step(dve.tensor_scalar(t, t, -0.5, 1.5, ALU.mult, ALU.add))
                ch.step(dve.tensor_tensor(y, t, r, ALU.mult))
                wide = y.unsqueeze(2).broadcast_to([P, width, DM])
                for o in outs[:-1]:
                    ch.mark(dve.tensor_tensor(o, xc, wide, ALU.mult))
                return dve.tensor_tensor(outs[-1], xc, wide, ALU.mult)
            LN_STEPS = 9

            for b in range(B):
                dve.wait_ge(sem(f"gathered_{b}"), 16 * TB)
                xb = x0[:, TB * b:TB * b + TB, :]
                ln_centre(xb, xc, sq, TB)
                ch.step(ln_scale(2 * b + 1, xc, TB, [u]))
                ln_centre(u, xc, sq, TB)
                ub = u2d[:, TB * b:TB * b + TB]
                ln_scale(2 * b + 2, xc, TB, [ub[:, :, 0, :], ub[:, :, 1, :]]).then_inc(sem("u2_ready"), 1)
                ch.mark(dve.tensor_tensor(xb, xb, u, ALU.add))

            dve.wait_ge(sem("c_weights_in"), 16 * (len(loads) - EARLY_LOADS))
            for d in range(2):
                ch.mark(dve.tensor_scalar(skip[:, d, :], ident[:], dskip[:, d:d + 1], None, ALU.mult))
            dve.wait_ge(sem("expA"), 4)
            ch.mark(dve.tensor_scalar(negA[:].rearrange("p a b c -> p (a b c)"),
                                      negA[:].rearrange("p a b c -> p (a b c)"), -1.0, None, ALU.mult))

            ch.wait()
            dve.memset(ohTb[E:E + 1, :], 1.0).then_inc(sem("constants_ready"), 1)

            def softplus_c(unit):
                dve.wait_ge(sem("softplus_l"), unit + 1)
                dve.scalar_tensor_tensor(e_, w_, -1.0, e_, ALU.add, ALU.subtract).then_inc(sem("sp_c"), 1)

            def dt_times_u(d, i, b):
                dve.wait_ge(sem("dt_ready"), 2 * i + b + 1)
                dve.tensor_tensor(du[:, b], dt[:, b], xs_at(d, i, b), ALU.mult).then_inc(sem("du_ready"), 1)

            def keep_last(g, d, b, q):
                dve.wait_ge(sem("scans"), g * NR + NR)
                dve.tensor_copy(carry[:, d, b, q], hs[:, q % 2, :, T - 1]).then_inc(sem("carried"), 1)

            def group_input(d, i, b, q):
                g = (2 * i + b) * NQ + q
                if q:
                    keep_last(g - 1, d, b, q - 1)
                elif not is_unit(i, b, 0):
                    keep_last(g - 1, 0 if is_unit(i, b, UPD) else d, 1 - b, NQ - 1)
                dve.wait_ge(sem("du_spread"), g + 1)
                if q == 0:
                    dve.wait_ge(sem(f"rep_in_{b}"), i * 64 + 64)
                dve.tensor_tensor(dbu, ps[:, 1, :].unsqueeze(1).broadcast_to([P, NR, T]), rep[:, b, 0],
                                  ALU.mult).then_inc(sem("dbu_ready"), 1)

            def group_scans(d, i, b, q):
                g = (2 * i + b) * NQ + q
                if not (isinstance(i, int) and i in (0, CB)):
                    dve.wait_ge(sem("carried"), g - 2 * NQ + 1)
                if not (is_unit(i, b, 0) and q < 2):
                    dve.wait_ge(sem("hc_ready"), g - 1)
                dve.wait_ge(sem("dbu_ready"), g + 1)
                for r in range(NR):
                    dve.wait_ge(sem("decay_ready"), g * NR + r + 1)
                    dve.tensor_tensor_scan(hs[:, q % 2, r], ps[:, bank(b, NR * q + r), :], dbu[:, r],
                                           carry[:, d, b, q, r:r + 1], ALU.mult, ALU.add) \
                       .then_inc(sem("scans"), 1)

            def y_by_z(d, i, b):
                unit = 2 * i + b
                dve.wait_ge(sem("summed"), unit * NQ + NQ)
                zc = z_at(d, i, b)
                dve.tensor_tensor(zc, ps[:, 6, :], zc, ALU.mult).then_inc(sem("yz_ready"), 1)

            def bc_out(m, d, i, b):
                k = b if isinstance(i, int) and i == 0 else d
                dve.wait_ge(sem("bc_ps"), m + 1)
                before = i * 2 + b - 1 if d == 0 else (i - CB) * 2 + b + 1
                dve.wait_ge(sem(f"bc_in_dram_{k}"), before * 16)
                dve.tensor_copy(bc_sb[:, k, :], ps[2 * NS * d:2 * NS * d + 2 * NS, SIDE, :]) \
                   .then_inc(sem("bc_in_sbuf"), 1)

            def c_front(s, m, j, bb):
                c = buffers(m)
                if s == 5:
                    dve.wait_ge(sem("dir_out"), m + 1)
                    if isinstance(m, int) and m == 0:
                        dve.wait_ge(sem("bc_in_dram_1"), 16 * (NCH + 1))
                    else:
                        dve.wait_ge(sem("attn_ps"), m)
                    dve.tensor_tensor(c.ga[:, 1], ps[:, c.side2, REV], gate[:, bass.ds(tokens(j, bb) * T, T)],
                                      ALU.mult).then_inc(sem("ga_backward"), 1)
                if s == 7:
                    dve.wait_ge(sem("attn_ps"), m + 1)
                    ch.wait()
                    dve.tensor_tensor(flat(c.h1), ps[:, c.side2, 0:TC * DM], flat(x0[:, bass.ds(tokens(j, bb) * TC, TC), :]),
                                      ALU.add).then_inc(sem("h1_sum"), 1)
                    dve.wait_ge(sem("h1_sum"), m + 1)
                    ln_centre(c.h1, c.xc, c.sq, TC)

            def c_middle(s, m, j, bb):
                c = buffers(m)
                if s == 1:
                    ln_scale(m + (NLN + 1), c.xc, TC, [c.xf]).then_inc(sem("xf_ready"), 1)
                if s == 5:
                    dve.wait_ge(sem("logits_read"), m + 1)
                    ch.step(dve.tensor_reduce(c.mx, c.lg, AX, ALU.max))
                    ch.step(dve.tensor_tensor(c.eq, c.lg, c.mx.unsqueeze(2).broadcast_to([P, TC, E]), ALU.is_equal))
                    ch.step(dve.tensor_tensor(c.eq, c.eq, rank[:].unsqueeze(1).broadcast_to([P, TC, E]), ALU.mult))
                    ch.step(dve.tensor_reduce(c.mx2, c.eq, AX, ALU.max))
                    dve.tensor_tensor(c.oh, c.eq, c.mx2.unsqueeze(2).broadcast_to([P, TC, E]), ALU.is_equal) \
                       .then_inc(sem("choice_ready"), 1)
                if s == 6 and not is_last(m):
                    dve.wait_ge(sem("fin_ready"), m + 1)
                    ch.mark(dve.tensor_copy(c.h1b, c.h1))
            C_MARKS = LN_STEPS + 5

            def c_end(s, m, j, bb):
                c = buffers(m)
                if s == 6:
                    dve.wait_ge(sem("moe_turned"), m + 1)
                    if not is_last(m):
                        dve.wait_ge(sem("out_done"), m * 16 + 16)
                    if isinstance(m, int) and m == NCH - 1:
                        ch.wait()
                    dve.tensor_tensor(c.fin.rearrange("p (h g) d -> p h g d", h=2),
                                      ps[:, c.moe, 0:TC * DM].rearrange("p (g h d) -> p h g d", h=2, d=DM),
                                      c.h1b.rearrange("p (h g) d -> p h g d", h=2), ALU.add) \
                       .then_inc(sem("fin_ready"), 1)

            def c_slot(i, b, s):
                for lag, step in ((3, c_end), (2, c_middle), (1, c_front)):
                    if c_chunk(i, b, lag):
                        step(s, *c_chunk(i, b, lag))

            def unit(d, i, b):
                for s in range(2 * NQ):
                    q = s // 2
                    if s % 2 == 0:
                        group_input(d, i, b, q)
                    else:
                        group_scans(d, i, b, q)
                    if s == 3:
                        if b:
                            y_by_z(d, i, 0)
                        elif not is_unit(i, b, 0):
                            y_by_z(0 if is_unit(i, b, UPD) else d, i - 1, 1)
                        if not is_unit(i, b, UNITS - 1):
                            softplus_c(2 * i + b + 1)
                    if d == 0 and s == 4 and len(a2_items(i, b)) == 2:
                        bc_out(*a2_items(i, b)[0])
                    if s == 5 and not is_unit(i, b, UNITS - 1):
                        dt_times_u(*follows(d, i, b))
                    if d == 0 or is_unit(i, b, UPD):
                        if s == 0 and a2_before(i, b):
                            bc_out(*a2_before(i, b))
                    if s == FORWARD and forward_before(d, i, b):
                        m, at = forward_before(d, i, b)
                        dve.wait_ge(sem("forward_out"), m + 1)
                        dve.tensor_tensor(z[:, 0, bass.ds(at, T)], ps[:, SIDE2, :], gate[:, bass.ds(at, T)],
                                          ALU.mult).then_inc(sem("forward_gated"), 1)
                    if d:
                        c_slot(i, b, s)
                if is_unit(i, b, UPD - 1):
                    dve.wait_ge(sem("summed"), NQ * UPD - 2)
                    ch.step(dve.memset(xfT[DM:DM + 1], 1.0))
                    dve.memset(fin, 0.0).then_inc(sem("out_done"), 16)
                    dve.wait_ge(sem("out_done"), 16)
                    dve.memset(ohTb[E:E + 1, :], 1.0).then_inc(sem("fin_ready"), 1)

            def loop(start, end, body):
                ch.loop(start, end, body, 2 * C_MARKS)

            softplus_c(0)
            dt_times_u(0, 0, 0)
            units(dve, unit, loop)
            y_by_z(1, NCH - 1, 1)
            ch.step(dve.memset(one_xfT[DM:DM + 1, :], 1.0))
            tail({END: c_end, MIDDLE: c_middle, FRONT: c_front})


_INS = ["x", "L0_tok_ple_table"] + ["L0_attn_" + n for n in (
    "ln_g", "ln_b", "in_w", "conv_w", "conv_b", "out_w")] + [
    f"L0_attn_{d}_{n}" for d in "fb" for n in (
        "in_w", "conv_w", "conv_b", "xproj_w", "dt_w", "dt_b", "Alog", "D", "out_w")] + [
    "L0_ffn_" + n for n in ("router_w", "router_b", "W1", "b1", "W2", "b2")]


def kernel(**inputs):
    import concourse.bacc as _bacc
    from concourse.bass_utils import run_bass_kernel_spmd as _run

    nc = _bacc.Bacc("TRN2", target_bir_lowering=False, num_devices=1)
    arrays, aps = {}, {}
    for name in _INS:
        a = np.ascontiguousarray(inputs[name])
        arrays[f"in_{name}"] = a
        aps[name] = nc.dram_tensor(f"in_{name}", a.shape, mybir.dt.from_np(a.dtype), kind="ExternalInput").ap()
    B, L = inputs["x"].shape
    out = nc.dram_tensor("out_h", (B, L, inputs["L0_attn_ln_g"].shape[0]), F32, kind="ExternalOutput").ap()
    build(nc, aps, out)
    r = _run(nc, [arrays], core_ids=[0])
    return r.results[0]["out_h"]
```
